# Optimizing a Trainium2 kernel written in Bass

```python
import numpy as np
import jax
import jax.numpy as jnp

def _softmax(x, axis=-1):
    return jax.nn.softmax(x, axis=axis)

def _gelu(x):
    return jax.nn.gelu(x, approximate=True)

def _silu(x):
    return jax.nn.silu(x)

def _sigmoid(x):
    return jax.nn.sigmoid(x)

def _layernorm(x, axis=-1, eps=1e-05):
    m = jnp.mean(x, axis=axis, keepdims=True)
    v = jnp.var(x, axis=axis, keepdims=True)
    return (x - m) / jnp.sqrt(v + eps)

def _scatter_add(tgt, idx, src, axis=0):
    return tgt.at[idx].add(src)

def _segment_sum(src, seg, n):
    return jax.ops.segment_sum(src, seg, n)
kernel_name = 'mk_flamingo_gated_d1_seqx_r8_3654a6'

def setup_inputs(seed: int=0):
    np.random.seed(seed)
    _w = jnp.asarray

    def _rec_inputs():
        import jax
        import jax.numpy as jnp
        _rk = jax.random.key(seed)
        x = 0.0001212 + 1 * jax.random.normal(jax.random.fold_in(_rk, 1), (8, 128, 256), jnp.float32)
        _lenS = 128 - jax.random.randint(jax.random.fold_in(_rk, 7), (8,), 0, max(1, 128 // 4) + 1, jnp.int32)
        _lenS2 = 128 - jax.random.randint(jax.random.fold_in(_rk, 8), (8,), 0, max(1, 128 // 4) + 1, jnp.int32)
        _ctx_2048P = jax.random.normal(jax.random.fold_in(_rk, 11), (8, 16, 256), jnp.float32)
        _ctx_2048c = jax.random.dirichlet(jax.random.fold_in(_rk, 511), 0.3 * jnp.ones((16,), jnp.float32), (8, 128))
        _ctx_2048t = jnp.einsum('bsk,bkd->bsd', _ctx_2048c, _ctx_2048P)
        _ctx_2048t = _ctx_2048t * jax.lax.rsqrt(jnp.mean(jnp.square(_ctx_2048t)) + 1e-12) * 0.953939
        ctx_2048 = 0.000173663 + 1.0001 * (_ctx_2048t + 0.3 * jax.random.normal(jax.random.fold_in(_rk, 611), (8, 128, 256), jnp.float32))
        _g = jax.random.normal(jax.random.fold_in(_rk, 9001), (2, 1), jnp.float32)
        _g = jnp.sign(_g) * jnp.maximum(jnp.abs(_g), 1.0) + (_g == 0) * 1.0
        g_xattn = _g[0]
        g_ffn = _g[1]
        return (x, ctx_2048, g_xattn, g_ffn)
    x, ctx_2048, g_xattn, g_ffn = _rec_inputs()

    def _L0_xattn_setup():
        import jax, jax.numpy as jnp
        import numpy as np
        B_DIM, T_DIM, C_DIM = (16, 128, 256)

        def _wkv(w, u, k, v):
            Bn, Tn, Cn = k.shape
            NEG_INF = jnp.float32(-1e+38)

            def step(carry, kv_t):
                p, q, o = carry
                kt, vt = kv_t
                no = jnp.maximum(o, u + kt)
                A = jnp.exp(o - no)
                E = jnp.exp(u + kt - no)
                y = (A * p + E * vt) / (A * q + E)
                no2 = jnp.maximum(w + o, kt)
                A2 = jnp.exp(w + o - no2)
                E2 = jnp.exp(kt - no2)
                return ((A2 * p + E2 * vt, A2 * q + E2, no2), y)
            init = (jnp.zeros((Bn, Cn), k.dtype), jnp.zeros((Bn, Cn), k.dtype), jnp.full((Bn, Cn), NEG_INF, k.dtype))
            kT = jnp.moveaxis(k, 1, 0)
            vT = jnp.moveaxis(v, 1, 0)
            _, yT = jax.lax.scan(step, init, (kT, vT))
            return jnp.moveaxis(yT, 0, 1)
        key = jax.random.key(seed)
        k1, k2, k3, k4 = jax.random.split(key, 4)
        w = -jnp.exp(jax.random.normal(k1, (C_DIM,), jnp.float32))
        u = jax.random.normal(k2, (C_DIM,), jnp.float32)
        k = jax.random.normal(k3, (B_DIM, T_DIM, C_DIM), jnp.float32)
        v = jax.random.normal(k4, (B_DIM, T_DIM, C_DIM), jnp.float32)
        return {'B': B_DIM, 'T': T_DIM, 'C': C_DIM, 'w': w, 'u': u, 'k': k, 'v': v}
    _L0_xattn_all = _L0_xattn_setup()
    _L0_xattn_in = {k: v for k, v in _L0_xattn_all.items() if k in ('w', 'u')}
    del _L0_xattn_all

    def _L0_ffn_setup():
        import jax, jax.numpy as jnp
        import numpy as np
        HIDDEN = 256
        INTER = 1024
        SCALE = 64.0

        def fwht(x):
            orig_shape = x.shape
            n = orig_shape[-1]
            x = x.reshape(-1, n)
            h = 1
            while h < n:
                x = x.reshape(-1, n // (2 * h), 2, h)
                a, b = (x[:, :, 0, :], x[:, :, 1, :])
                x = jnp.stack([a + b, a - b], axis=2).reshape(-1, n)
                h *= 2
            return (x / jnp.sqrt(jnp.asarray(n, x.dtype))).reshape(orig_shape)
        key = jax.random.key(seed)
        ks = jax.random.split(key, 8)
        inp = jax.random.normal(ks[0], (4, 256, HIDDEN), dtype=jnp.float32)
        SU_ug = jnp.where(jax.random.bernoulli(ks[1], 0.5, (HIDDEN,)), 1.0, -1.0).astype(jnp.float32)
        SU_dp = jnp.where(jax.random.bernoulli(ks[2], 0.5, (INTER,)), 1.0, -1.0).astype(jnp.float32)
        Wscale_ug = jax.random.uniform(ks[3], (2 * INTER,), jnp.float32, 0.5, 1.5)
        Wscale_dp = jax.random.uniform(ks[4], (HIDDEN,), jnp.float32, 0.5, 1.5)
        W_up = jax.random.normal(ks[5], (INTER, HIDDEN), dtype=jnp.float32) * 0.02
        W_gate = jax.random.normal(ks[6], (INTER, HIDDEN), dtype=jnp.float32) * 0.02
        W_down = jax.random.normal(ks[7], (HIDDEN, INTER), dtype=jnp.float32) * 0.02
        return {'input': inp, 'SU_ug': SU_ug, 'SU_dp': SU_dp, 'Wscale_ug': Wscale_ug, 'Wscale_dp': Wscale_dp, 'W_up': W_up, 'W_gate': W_gate, 'W_down': W_down}
    _L0_ffn_all = _L0_ffn_setup()
    _L0_ffn_in = {k: v for k, v in _L0_ffn_all.items() if k in ('SU_ug', 'SU_dp', 'Wscale_ug', 'Wscale_dp', 'W_up', 'W_gate', 'W_down')}
    del _L0_ffn_all
    return {'x': x, 'ctx_2048': ctx_2048, 'g_xattn': g_xattn, 'g_ffn': g_ffn, 'L0_xattn_w': _L0_xattn_in['w'], 'L0_xattn_u': _L0_xattn_in['u'], 'L0_ffn_SU_ug': _L0_ffn_in['SU_ug'], 'L0_ffn_SU_dp': _L0_ffn_in['SU_dp'], 'L0_ffn_Wscale_ug': _L0_ffn_in['Wscale_ug'], 'L0_ffn_Wscale_dp': _L0_ffn_in['Wscale_dp'], 'L0_ffn_W_up': _L0_ffn_in['W_up'], 'L0_ffn_W_gate': _L0_ffn_in['W_gate'], 'L0_ffn_W_down': _L0_ffn_in['W_down']}

def reference(x, ctx_2048, g_xattn, g_ffn, L0_xattn_w, L0_xattn_u, L0_ffn_SU_ug, L0_ffn_SU_dp, L0_ffn_Wscale_ug, L0_ffn_Wscale_dp, L0_ffn_W_up, L0_ffn_W_gate, L0_ffn_W_down):
    import jax
    import jax.numpy as jnp

    def _L0_xattn_ref(B, T, C, w, u, k, v):
        import jax, jax.numpy as jnp
        import numpy as np
        B_DIM, T_DIM, C_DIM = (16, 128, 256)

        def _wkv(w, u, k, v):
            Bn, Tn, Cn = k.shape
            NEG_INF = jnp.float32(-1e+38)

            def step(carry, kv_t):
                p, q, o = carry
                kt, vt = kv_t
                no = jnp.maximum(o, u + kt)
                A = jnp.exp(o - no)
                E = jnp.exp(u + kt - no)
                y = (A * p + E * vt) / (A * q + E)
                no2 = jnp.maximum(w + o, kt)
                A2 = jnp.exp(w + o - no2)
                E2 = jnp.exp(kt - no2)
                return ((A2 * p + E2 * vt, A2 * q + E2, no2), y)
            init = (jnp.zeros((Bn, Cn), k.dtype), jnp.zeros((Bn, Cn), k.dtype), jnp.full((Bn, Cn), NEG_INF, k.dtype))
            kT = jnp.moveaxis(k, 1, 0)
            vT = jnp.moveaxis(v, 1, 0)
            _, yT = jax.lax.scan(step, init, (kT, vT))
            return jnp.moveaxis(yT, 0, 1)
        return _wkv(w, u, k, v)

    def _L0_ffn_ref(input, SU_ug, SU_dp, Wscale_ug, Wscale_dp, W_up, W_gate, W_down):
        import jax, jax.numpy as jnp
        import numpy as np
        HIDDEN = 256
        INTER = 1024
        SCALE = 64.0

        def fwht(x):
            orig_shape = x.shape
            n = orig_shape[-1]
            x = x.reshape(-1, n)
            h = 1
            while h < n:
                x = x.reshape(-1, n // (2 * h), 2, h)
                a, b = (x[:, :, 0, :], x[:, :, 1, :])
                x = jnp.stack([a + b, a - b], axis=2).reshape(-1, n)
                h *= 2
            return (x / jnp.sqrt(jnp.asarray(n, x.dtype))).reshape(orig_shape)
        n = SU_ug.shape[0]
        x = input.reshape(-1, n)
        x = fwht(x * SU_ug) / SCALE
        x_up = x @ W_up.T * (Wscale_ug[:INTER] * SCALE)
        x_gate = x @ W_gate.T * (Wscale_ug[INTER:] * SCALE)
        x = jax.nn.silu(x_gate) * x_up
        x = fwht(x * SU_dp) / SCALE
        x = x @ W_down.T * (Wscale_dp * SCALE)
        return x.reshape(input.shape)
    x = x + jnp.tanh(g_xattn[0]) * _L0_xattn_ref(8, 128, 256, L0_xattn_w, L0_xattn_u, _layernorm(x, axis=-1), ctx_2048)
    x = x + jnp.tanh(g_ffn[0]) * _L0_ffn_ref(_layernorm(x, axis=-1), L0_ffn_SU_ug, L0_ffn_SU_dp, L0_ffn_Wscale_ug, L0_ffn_Wscale_dp, L0_ffn_W_up, L0_ffn_W_gate, L0_ffn_W_down)
    return x

_drawn_inputs = setup_inputs


def setup_inputs(seed=0):
    import zlib

    import numpy as np

    out = dict(_drawn_inputs(seed))
    spreads = {}
    factors = {'L0_ffn_Wscale_ug': 4.89, 'L0_ffn_Wscale_dp': 6.726}
    for name, (base, spread) in spreads.items():
        noise = np.random.default_rng([zlib.crc32(name.encode()), seed]).standard_normal(out[name].shape)
        drawn = base * np.exp(spread * noise) if base else spread * noise
        out[name] = jnp.asarray(drawn.astype(out[name].dtype))
    for name, factor in factors.items():
        out[name] = (out[name] * factor).astype(out[name].dtype)
    return out
```

```python
from contextlib import ExitStack

import concourse.bass as bass
from concourse import mybir

F32 = mybir.dt.float32
F32R = mybir.dt.float32r
ALU = mybir.AluOpType
ACT = mybir.ActivationFunctionType

P = 128
NB = 8
C = 256
INTER = 1024
CT = C // P
JT = INTER // P
GB = 2
NG = NB // GB
GT = GB * P
PAD = P + 1
EPS = 1e-5
CLAMP = 60.0
SCALE_UG = C ** -0.5
SCALE_DP = 0.5 * INTER ** -0.5

V_W, V_U, V_SUG, V_SDP, V_SUP, V_SGATE, V_SOUT = 0, 2, 4, 6, 14, 22, 30
NV = 32

NBANKS = 4
UG_FILLS = 2 * JT * CT // 4
DT_FILLS = JT * CT // 4
DM_FILLS = JT // 2
PREP = UG_FILLS + DT_FILLS + DM_FILLS
LAG = 2

FRONT_SLOTS = {0: ["norm1"], 1: ["keys"], 2: ["wkv"], 3: ["quotient"], 5: ["residual"], 6: ["turn"], 7: ["fwht"]}


def build(nc, x, ctx, vecs, gates, consts, steps, w_up, w_gate, w_down, out):
    with ExitStack() as stack:
        def sb(name, shape, dt=F32):
            return stack.enter_context(nc.sbuf_tensor(name, shape, dt))

        def bank(name):
            return stack.enter_context(nc.psum_tensor(name, [P, 512], F32))

        def sem(name):
            return stack.enter_context(nc.semaphore(name))

        X = sb("X", [P, NB, C])
        V = sb("V", [P, GB, C])
        VR = sb("VR", [NV, P])
        VT = sb("VT", [P, NV])
        WR = sb("WR", [P, C])
        GATE = sb("GATE", [P, 2])
        TG = sb("TG", [P, 2])
        HI = sb("HI", [P, 2 * P])
        HP = sb("HP", [P, P], F32R)
        HN = sb("HN", [P, P], F32R)
        STEP = sb("STEP", [P, GT])
        STEPR = sb("STEPR", [P, GT], F32R)
        NEGW = sb("NEGW", [P, C])
        WPLUS = sb("WPLUS", [P, C], F32R)
        DEC = sb("DEC", [P, CT])
        CUR = sb("CUR", [P, CT])
        TMPU = sb("TMPU", [P, CT])
        RATIO = sb("RATIO", [P, CT])
        NEGM = sb("NEGM", [P, CT])
        D = sb("D", [P, CT, GB * PAD])
        ALPHA = sb("ALPHA", [P, JT])
        HALFG = sb("HALFG", [P, JT])
        OUTS = sb("OUTS", [P, CT])
        NHALF = sb("NHALF", [P, GB])
        EPST = sb("EPST", [P, GB])
        SCRATCH = sb("SCRATCH", [P, 1])
        WN = sb("WN", [P, 2, JT, C])
        WTH = sb("WTH", [P, 2, JT, CT, P], F32R)
        WTL = sb("WTL", [P, 2, JT, CT, P], F32R)
        DN = sb("DN", [P, CT, JT, P])
        DB = sb("DB", [P, CT, JT, P])
        DTH = sb("DTH", [P, JT, C], F32R)
        DTL = sb("DTL", [P, JT, C], F32R)
        MH = sb("MH", [P, JT, C], F32R)
        ML = sb("ML", [P, JT, C], F32R)
        BS1 = sb("BS1", [P, GB, 6]); MV1 = sb("MV1", [P, GB, 2]); VE1 = sb("VE1", [P, GB]); RS1 = sb("RS1", [P, GB])
        BS2 = sb("BS2", [P, GB, 6]); MV2 = sb("MV2", [P, GB, 2]); VE2 = sb("VE2", [P, GB]); RS2 = sb("RS2", [P, GB])
        XHAT = sb("XHAT", [P, GB, C])
        Z = sb("Z", [P, GB, C])
        EA = sb("EA", [P, CT, GB, PAD])
        EV = sb("EV", [P, CT, GB, PAD])
        SQ = sb("SQ", [P, CT, GB, PAD])
        SP_ = sb("SP_", [P, CT, GB, PAD])
        NUM = sb("NUM", [P, CT, GB, P])
        DEN = sb("DEN", [P, CT, GB, P])
        REC = sb("REC", [P, CT, GB, P])
        Y = sb("Y", [P, CT, GB, P])
        ZH = sb("ZH", [P, CT, GT], F32R)
        ZL = sb("ZL", [P, CT, GT], F32R)
        FH = sb("FH", [P, NG, CT, GT], F32R)
        FL = sb("FL", [P, NG, CT, GT], F32R)
        T = sb("T", [P, JT, GT])
        G1 = sb("G1", [P, JT, GT])
        H = sb("H", [P, JT, GT])
        HH = sb("HH", [P, JT, GT], F32R)
        HL = sb("HL", [P, JT, GT], F32R)

        UG = [bank(f"UG{i}") for i in range(NBANKS)]
        OD = bank("OD")
        KZ = bank("KZ")
        VX = bank("VX")
        YB = bank("YB")
        IDENT = HI[:, P:2 * P]

        x0_in = sem("x0_in"); x1_in = sem("x1_in"); ctx_in = sem("ctx_in"); const_in = sem("const_in")
        vec_in = sem("vec_in"); row_in = sem("row_in"); gate_in = sem("gate_in")
        wug_in = [sem(f"wug{i}_in") for i in range(2)]
        wd_in = sem("wd_in"); stored = sem("stored")
        cleared = sem("cleared"); pads = sem("pads"); vecs_turned = sem("vecs_turned"); vecs_kept = sem("vecs_kept")
        small = sem("small"); tanh_gate = sem("tanh_gate"); exps = sem("exps"); decay_set = sem("decay_set")
        consts_r = sem("consts_r"); wplus = sem("wplus"); rows_clear = sem("rows_clear"); halves = sem("halves")
        bank_full = sem("bank_full"); bank_hi = sem("bank_hi"); bank_read = sem("bank_read")
        wd_scaled = sem("wd_scaled"); fly_p = sem("fly_p"); fly_v = sem("fly_v")
        stats1 = sem("stats1"); mv1 = sem("mv1"); ve1 = sem("ve1"); rstd1 = sem("rstd1"); xhat = sem("xhat")
        k_turned = sem("k_turned"); v_turned = sem("v_turned"); a_ready = sem("a_ready"); av_ready = sem("av_ready")
        scanned = sem("scanned"); mixed = sem("mixed"); recip = sem("recip"); y_ready = sem("y_ready")
        y_turned = sem("y_turned"); x1_ready = sem("x1_ready"); stats2 = sem("stats2"); mv2 = sem("mv2")
        ve2 = sem("ve2"); rstd2 = sem("rstd2"); z_ready = sem("z_ready"); z_turned = sem("z_turned")
        z_hi = sem("z_hi"); z_lo = sem("z_lo"); f_full = sem("f_full"); f_hi = sem("f_hi"); f_lo = sem("f_lo")
        t_ready = sem("t_ready"); g_ready = sem("g_ready"); h_hi = sem("h_hi"); h_lo = sem("h_lo")
        down_full = sem("down_full"); out_ready = sem("out_ready")

        wd_v = w_down.rearrange("(t p) (j q) -> p t j q", p=P, q=P)
        x_v = x.rearrange("b p c -> p b c")
        ctx_v = ctx.rearrange("b p c -> p b c")
        out_v = out.rearrange("b p c -> p b c")

        def fill(n):
            return UG[n % NBANKS]

        block = stack.enter_context(nc.Block())

        @block.sync
        def _(sp):
            sp.dma_start(X[:, 0:GB, :], x_v[:, 0:GB, :]).then_inc(x0_in, 16)
            sp.dma_start(HI[:, :], consts).then_inc(const_in, 16)
            sp.dma_start(VR[:, :], vecs).then_inc(vec_in, 16)
            sp.dma_start(V[:, :, :], ctx_v[:, 0:GB, :]).then_inc(ctx_in, 16)
            sp.dma_start(GATE[:, :], gates).then_inc(gate_in, 16)
            sp.wait_ge(rows_clear, 2)
            w_row = vecs[V_W:V_W + CT, :].rearrange("(o a) b -> o (a b)", o=1)
            for r in (0, 32):
                sp.dma_start(WR[r:r + 1, :], w_row).then_inc(row_in, 16)
                sp.dma_start(STEP[r:r + 1, :], steps).then_inc(row_in, 16)
            for i, w in enumerate((w_gate, w_up)):
                sp.dma_start(WN[:, i, :, :], w.rearrange("(t p) c -> p t c", p=P)).then_inc(wug_in[i], 16)
            for t in range(CT):
                sp.dma_start(DN[:, t, :, :], wd_v[:, t, :, :]).then_inc(wd_in, 16)
            sp.dma_start(X[:, GB:NB, :], x_v[:, GB:NB, :]).then_inc(x1_in, 16)
            sp.wait_ge(v_turned, 1)
            sp.dma_start(V[:, :, :], ctx_v[:, GB:2 * GB, :]).then_inc(ctx_in, 16)

            def store(g):
                sp.wait_ge(out_ready, g + 2)
                sp.dma_start(out_v[:, bass.ds(GB * g, GB), :], X[:, bass.ds(GB * g, GB), :]).then_inc(stored, 16)

            with sp.Fori(0, NG - 2) as g:
                sp.wait_ge(v_turned, g + 2)
                sp.dma_start(V[:, :, :], ctx_v[:, bass.ds(GB * g + 2 * GB, GB), :]).then_inc(ctx_in, 16)
                store(g)
            store(NG - 2)
            store(NG - 1)
            sp.wait_ge(stored, 16 * NG)

        @block.gpsimd
        def _(pool):
            pool.memset(WR[:, :], 0.0).then_inc(rows_clear, 1)
            pool.memset(STEP[:, :], 0.0).then_inc(rows_clear, 1)
            pool.memset(NHALF[:, :], -0.5).then_inc(cleared, 1)
            pool.memset(EPST[:, :], EPS).then_inc(cleared, 1)
            pool.memset(EA[:, :, :, :], 0.0).then_inc(pads, 1)
            pool.memset(EV[:, :, :, :], 0.0).then_inc(pads, 1)
            pool.memset(D[:, :, :], 0.0).then_inc(cleared, 1)

            def rstd(g, mv, MV, ve, VE, rs, RS):
                pool.wait_ge(mv, g + 1)
                pool.tensor_tensor(VE[:, :], MV[:, :, 1], EPST[:, :], ALU.add).then_inc(ve, 1)
                pool.wait_ge(ve, g + 1)
                pool.tensor_tensor(RS[:, :], VE[:, :], NHALF[:, :], ALU.pow).then_inc(rs, 1)

            def front(stage, g):
                if stage == "norm1":
                    rstd(g, mv1, MV1, ve1, VE1, rstd1, RS1)
                elif stage == "residual":
                    rstd(g, mv2, MV2, ve2, VE2, rstd2, RS2)

            def butterflies(t, step):
                src, dst = (DN, DB) if step % 2 == 0 else (DB, DN)
                h = 1 << step
                s = src[:, t, :, :].rearrange("p (n two h) q -> p n two (h q)", two=2, h=h)
                d = dst[:, t, :, :].rearrange("p (n two h) q -> p n two (h q)", two=2, h=h)
                return s, d

            pool.wait_ge(cleared, 2)
            front("norm1", 0)

            def fly(step):
                s, d = butterflies(0, step)
                pool.wait_ge(wd_scaled, 1)
                if step:
                    pool.wait_ge(fly_p, 2 * step)
                pool.tensor_tensor(d[:, :, 0, :], s[:, :, 0, :], s[:, :, 1, :], ALU.add).then_inc(fly_p, 1)
                pool.tensor_tensor(d[:, :, 1, :], s[:, :, 0, :], s[:, :, 1, :], ALU.subtract).then_inc(fly_p, 1)

            fly(0)
            fly(1)
            front("residual", 0)
            fly(2)

            def ffn(g, nxt):
                for j in range(JT):
                    for stage in FRONT_SLOTS.get(j, []) if nxt is not None else []:
                        front(stage, nxt)
                    pool.wait_ge(h_hi, g * JT + j + 1)
                    pool.tensor_tensor(HL[:, j, :], H[:, j, :], HH[:, j, :].bitcast(F32), ALU.subtract).then_inc(h_lo, 1)

            with pool.Fori(0, NG - 1) as g:
                ffn(g, g + 1)
            ffn(NG - 1, None)

        @block.scalar
        def _(act):
            def copy_hi(dst, src):
                return act.activation(dst, src, ACT.Copy)

            def front(stage, g):
                if stage == "keys":
                    act.wait_ge(k_turned, g + 1)
                    for t in range(CT):
                        i = act.activation(EA[:, t, :, 1:PAD], KZ[:, t * GT:(t + 1) * GT].rearrange("p (b q) -> p b q", b=GB),
                                           ACT.Exp, bias=NEGM[:, t:t + 1])
                    i.then_inc(a_ready, 1)
                elif stage == "turn":
                    act.wait_ge(z_turned, g + 1)
                    for t in range(CT):
                        i = act.activation(ZH[:, t, :], KZ[:, t * GT:(t + 1) * GT], ACT.Copy, scale=VT[:, V_SUG + t:V_SUG + t + 1])
                    i.then_inc(z_hi, 1)
                elif stage == "fwht":
                    act.wait_ge(f_full, g + 1)
                    act.activation(FH[:, bass.ds(g, 1), :, :], VX[:, :].rearrange("p (o t n) -> p o t n", o=1, t=CT),
                                   ACT.Copy, scale=SCALE_UG).then_inc(f_hi, 1)

            act.wait_ge(gate_in, 16)
            act.activation(TG[:, :], GATE[:, :], ACT.Tanh).then_inc(tanh_gate, 1)
            act.wait_ge(small, 3)
            act.activation(DEC[:, :], DEC[:, :], ACT.Exp).then_inc(exps, 1)
            act.activation(RATIO[:, :], CUR[:, :], ACT.Exp).then_inc(exps, 1)
            act.wait_ge(small, 5)
            act.wait_ge(pads, 1)
            front("keys", 0)

            def prep_hi(n):
                act.wait_ge(bank_full, n + 1)
                copy_hi(WTH[:, :, :, :, :].rearrange("p m j t q -> p (m j t q)")[:, 512 * n:512 * (n + 1)], fill(n)[:, :]).then_inc(bank_hi, 1)

            for n in range(UG_FILLS):
                prep_hi(n)
                if n == UG_FILLS // 2 - 1:
                    act.wait_ge(small, 10)
                    for t in range(CT):
                        act.wait_ge(wd_in, 16 * CT)
                        act.activation(DN[:, t, :, :], DN[:, t, :, :], ACT.Copy, scale=OUTS[:, t:t + 1]).then_inc(wd_scaled, 1)
            front("turn", 0)
            front("fwht", 0)
            for n in range(DT_FILLS):
                act.wait_ge(bank_full, UG_FILLS + n + 1)
                copy_hi(DTH[:, 2 * n:2 * n + 2, :].rearrange("p j c -> p (j c)"), fill(UG_FILLS + n)[:, :]).then_inc(bank_hi, 1)
            for n in range(DM_FILLS):
                m = UG_FILLS + DT_FILLS + n
                act.wait_ge(bank_full, m + 1)
                for i in range(2):
                    a = act.activation(MH[:, 2 * n + i, :], fill(m)[:, i * C:(i + 1) * C], ACT.Copy, scale=ALPHA[:, 2 * n + i:2 * n + i + 1])
                a.then_inc(bank_hi, 1)

            def ffn(g, nxt):
                def hi(j):
                    act.wait_ge(bank_read, PREP + g * JT + j + 1)
                    copy_hi(HH[:, j, :], H[:, j, :]).then_inc(h_hi, 1)

                for j in range(JT):
                    act.wait_ge(bank_full, PREP + g * JT + j + 1)
                    act.activation(T[:, j, :], fill(j)[:, 0:GT], ACT.Tanh, scale=HALFG[:, j:j + 1]).then_inc(t_ready, 1)
                    if j:
                        hi(j - 1)
                    for stage in FRONT_SLOTS.get(j, []) if nxt is not None else []:
                        if j == JT - 1:
                            hi(j)
                        front(stage, nxt)
                if nxt is None:
                    hi(JT - 1)

            with act.Fori(0, NG - 1) as g:
                ffn(g, g + 1)
            ffn(NG - 1, None)

        @block.vector
        def _(dve):
            def norm_stats(src, BS, stats, MV, mv, g):
                for b in range(GB):
                    dve.bn_stats(BS[:, b, :], src(b)).then_inc(stats, 1)
                dve.wait_ge(stats, (g + 1) * GB)
                dve.memset(SCRATCH[:, :], 0.0)
                for b in range(GB):
                    i = dve.bn_aggr(MV[:, b, :], BS[:, b, :])
                i.then_inc(mv, 1)

            def front(stage, g, first=False):
                def xb(b):
                    return X[:, bass.ds(GB * g + b, 1), :]

                if stage == "norm1":
                    dve.wait_ge(x0_in if first else x1_in, 16)
                    norm_stats(xb, BS1, stats1, MV1, mv1, g)
                    dve.wait_ge(rstd1, g + 1)
                    for b in range(GB):
                        i = dve.tensor_scalar(XHAT[:, b:b + 1, :], xb(b), MV1[:, b, 0:1], RS1[:, b:b + 1], ALU.subtract, ALU.mult)
                    i.then_inc(xhat, 1)
                elif stage == "wkv":
                    dve.wait_ge(a_ready, g + 1)
                    dve.wait_ge(v_turned, g + 1)
                    dve.tensor_tensor(EV[:, :, :, 1:PAD].rearrange("p t b q -> p (t b) q"), EA[:, :, :, 1:PAD].rearrange("p t b q -> p (t b) q"),
                                      VX[:, :].rearrange("p (n q) -> p n q", q=P), ALU.mult).then_inc(av_ready, 1)
                    flat = "p t b q -> p (t b q)"
                    dve.tensor_tensor_scan(SQ[:, :, :, :].rearrange(flat), D[:, :, :].rearrange("p t n -> p (t n)"), EA[:, :, :, :].rearrange(flat),
                                           0.0, ALU.mult, ALU.add).then_inc(scanned, 1)
                    dve.wait_ge(av_ready, g + 1)
                    dve.tensor_tensor_scan(SP_[:, :, :, :].rearrange(flat), D[:, :, :].rearrange("p t n -> p (t n)"), EV[:, :, :, :].rearrange(flat),
                                           0.0, ALU.mult, ALU.add).then_inc(scanned, 1)
                elif stage == "quotient":
                    for n, (dst, cur, state) in enumerate(((DEN, EA, SQ), (NUM, EV, SP_))):
                        dve.wait_ge(scanned, 2 * g + n + 1)
                        for t in range(CT):
                            i = dve.scalar_tensor_tensor(out=dst[:, t, :, :], in0=cur[:, t, :, 1:PAD], scalar=RATIO[:, t:t + 1],
                                                         in1=state[:, t, :, 0:P], op0=ALU.mult, op1=ALU.add)
                        i.then_inc(mixed, 1)
                    dve.wait_ge(mixed, 2 * g + 2)
                    dve.reciprocal(REC[:, :, :, :], DEN[:, :, :, :]).then_inc(recip, 1)
                    dve.wait_ge(recip, g + 1)
                    dve.tensor_tensor(Y[:, :, :, :], NUM[:, :, :, :], REC[:, :, :, :], ALU.mult).then_inc(y_ready, 1)
                elif stage == "residual":
                    dve.wait_ge(y_turned, g + 1)
                    xg = X[:, bass.ds(GB * g, GB), :]
                    dve.scalar_tensor_tensor(out=xg, in0=YB[:, :].rearrange("p (b c) -> p b c", b=GB), scalar=TG[:, 0:1], in1=xg,
                                             op0=ALU.mult, op1=ALU.add).then_inc(x1_ready, 1)
                    dve.wait_ge(x1_ready, g + 1)
                    dve.memset(SCRATCH[:, :], 0.0)
                    norm_stats(xb, BS2, stats2, MV2, mv2, g)
                    dve.wait_ge(rstd2, g + 1)
                    for b in range(GB):
                        i = dve.tensor_scalar(Z[:, b:b + 1, :], xb(b), MV2[:, b, 0:1], RS2[:, b:b + 1], ALU.subtract, ALU.mult)
                    i.then_inc(z_ready, 1)
                elif stage == "turn":
                    dve.wait_ge(z_hi, g + 1)
                    for t in range(CT):
                        i = dve.scalar_tensor_tensor(out=ZL[:, t, :], in0=KZ[:, t * GT:(t + 1) * GT], scalar=VT[:, V_SUG + t:V_SUG + t + 1],
                                                     in1=ZH[:, t, :].bitcast(F32), op0=ALU.mult, op1=ALU.subtract)
                    i.then_inc(z_lo, 1)
                elif stage == "fwht":
                    dve.wait_ge(f_hi, g + 1)
                    dve.scalar_tensor_tensor(out=FL[:, bass.ds(g, 1), :, :].rearrange("p o t n -> p (o t n)"), in0=VX[:, :], scalar=SCALE_UG,
                                             in1=FH[:, bass.ds(g, 1), :, :].rearrange("p o t n -> p (o t n)").bitcast(F32),
                                             op0=ALU.mult, op1=ALU.subtract).then_inc(f_lo, 1)

            front("norm1", 0, first=True)

            dve.wait_ge(const_in, 16)
            dve.tensor_copy(HP[:, :], HI[:, 0:P]).then_inc(consts_r, 1)
            dve.tensor_scalar(HN[:, :], HI[:, 0:P], -1.0, None, ALU.mult).then_inc(consts_r, 1)
            dve.wait_ge(vecs_turned, 1)
            dve.tensor_copy(VT[:, :], YB[:, 0:NV]).then_inc(vecs_kept, 1)
            dve.wait_ge(vecs_kept, 1)
            dve.tensor_scalar(DEC[:, :], VT[:, V_W:V_W + CT], 0.0, None, ALU.min).then_inc(small, 1)
            dve.tensor_scalar(TMPU[:, :], VT[:, V_W:V_W + CT], 0.0, None, ALU.max).then_inc(small, 1)
            dve.wait_ge(small, 2)
            dve.tensor_tensor(NEGM[:, :], TMPU[:, :], VT[:, V_U:V_U + CT], ALU.add).then_inc(halves, 1)
            dve.wait_ge(halves, 1)
            dve.tensor_scalar(CUR[:, :], NEGM[:, :], CLAMP, -CLAMP, ALU.min, ALU.max).then_inc(small, 1)
            dve.wait_ge(small, 3)
            dve.tensor_scalar(NEGM[:, :], CUR[:, :], 0.0, -1.0, ALU.max, ALU.mult).then_inc(small, 2)
            dve.wait_ge(row_in, 64)
            dve.tensor_scalar(NEGW[:, :], WR[:, :], 0.0, -1.0, ALU.max, ALU.mult).then_inc(wplus, 1)
            dve.tensor_copy(STEPR[:, :], STEP[:, :]).then_inc(wplus, 1)
            dve.wait_ge(wplus, 1)
            dve.tensor_copy(WPLUS[:, :], NEGW[:, :]).then_inc(wplus, 1)
            dve.wait_ge(wplus, 3)
            dve.tensor_tensor(WPLUS[32:33, :], NEGW[32:33, :], WPLUS[32:33, :].bitcast(F32), ALU.subtract).then_inc(wplus, 1)
            dve.wait_ge(vecs_kept, 1)
            dve.tensor_scalar(HALFG[:, :], VT[:, V_SGATE:V_SGATE + JT], 0.5, None, ALU.mult).then_inc(small, 1)
            dve.scalar_tensor_tensor(out=ALPHA[:, :], in0=VT[:, V_SUP:V_SUP + JT], scalar=SCALE_DP, in1=VT[:, V_SGATE:V_SGATE + JT],
                                     op0=ALU.mult, op1=ALU.mult).then_inc(small, 1)
            dve.wait_ge(small, 7)
            dve.tensor_tensor(ALPHA[:, :], ALPHA[:, :], VT[:, V_SDP:V_SDP + JT], ALU.mult).then_inc(small, 1)
            dve.wait_ge(tanh_gate, 1)
            dve.tensor_scalar(OUTS[:, :], VT[:, V_SOUT:V_SOUT + CT], TG[:, 1:2], None, ALU.mult).then_inc(small, 2)
            dve.wait_ge(exps, 1)
            dve.wait_ge(cleared, 3)
            for t in range(CT):
                i = dve.tensor_scalar(D[:, t, :].rearrange("p (b q) -> p b q", b=GB)[:, :, 1:PAD], D[:, t, :].rearrange("p (b q) -> p b q", b=GB)[:, :, 1:PAD],
                                      0.0, DEC[:, t:t + 1], ALU.mult, ALU.add)
            i.then_inc(decay_set, 1)

            def prep_lo(n):
                dve.wait_ge(bank_hi, n + 1)
                view = "p m j t q -> p (m j t q)"
                dve.tensor_tensor(WTL[:, :, :, :, :].rearrange(view)[:, 512 * n:512 * (n + 1)], fill(n)[:, :],
                                  WTH[:, :, :, :, :].rearrange(view)[:, 512 * n:512 * (n + 1)].bitcast(F32), ALU.subtract).then_inc(bank_read, 1)

            def fly(step):
                src, dst = (DN, DB) if step % 2 == 0 else (DB, DN)
                s = src[:, 1, :, :].rearrange("p (n two h) q -> p n two (h q)", two=2, h=1 << step)
                d = dst[:, 1, :, :].rearrange("p (n two h) q -> p n two (h q)", two=2, h=1 << step)
                dve.wait_ge(wd_scaled, 2)
                if step:
                    dve.wait_ge(fly_v, 2 * step)
                dve.tensor_tensor(d[:, :, 0, :], s[:, :, 0, :], s[:, :, 1, :], ALU.add).then_inc(fly_v, 1)
                dve.tensor_tensor(d[:, :, 1, :], s[:, :, 0, :], s[:, :, 1, :], ALU.subtract).then_inc(fly_v, 1)

            dve.wait_ge(pads, 2)
            dve.wait_ge(decay_set, 1)
            dve.wait_ge(exps, 2)
            front("wkv", 0)
            front("quotient", 0)
            prep_lo(0)
            front("residual", 0)
            prep_lo(1)
            prep_lo(2)
            prep_lo(3)
            fly(0)
            for n in range(4, UG_FILLS):
                prep_lo(n)
            front("turn", 0)
            front("fwht", 0)
            fly(1)
            fly(2)
            for n in range(DT_FILLS):
                dve.wait_ge(bank_hi, UG_FILLS + n + 1)
                v = "p j c -> p (j c)"
                dve.tensor_tensor(DTL[:, 2 * n:2 * n + 2, :].rearrange(v), fill(UG_FILLS + n)[:, :],
                                  DTH[:, 2 * n:2 * n + 2, :].rearrange(v).bitcast(F32), ALU.subtract).then_inc(bank_read, 1)
            for n in range(DM_FILLS):
                m = UG_FILLS + DT_FILLS + n
                dve.wait_ge(bank_hi, m + 1)
                for i in range(2):
                    j = 2 * n + i
                    a = dve.scalar_tensor_tensor(out=ML[:, j, :], in0=fill(m)[:, i * C:(i + 1) * C], scalar=ALPHA[:, j:j + 1],
                                                 in1=MH[:, j, :].bitcast(F32), op0=ALU.mult, op1=ALU.subtract)
                a.then_inc(bank_read, 1)

            dve.memset(SCRATCH[:, :], 0.0).then_inc(out_ready, 1)

            def ffn(g, nxt):
                for j in range(JT):
                    dve.wait_ge(t_ready, g * JT + j + 1)
                    dve.scalar_tensor_tensor(out=G1[:, j, :], in0=T[:, j, :], scalar=1.0, in1=fill(j)[:, 0:GT], op0=ALU.add,
                                             op1=ALU.mult).then_inc(g_ready, 1)
                    dve.wait_ge(g_ready, g * JT + j + 1)
                    dve.tensor_tensor(H[:, j, :], G1[:, j, :], fill(j)[:, GT:2 * GT], ALU.mult).then_inc(bank_read, 1)
                    for stage in FRONT_SLOTS.get(j, []) if nxt is not None else []:
                        front(stage, nxt)
                dve.wait_ge(down_full, g + 1)
                xg = X[:, bass.ds(GB * g, GB), :]
                dve.tensor_tensor(xg, OD[:, :].rearrange("p (b c) -> p b c", b=GB), xg, ALU.add).then_inc(out_ready, 1)

            with dve.Fori(0, NG - 1) as g:
                ffn(g, g + 1)
            ffn(NG - 1, None)

        @block.tensor
        def _(pe):
            def front(stage, g):
                if stage == "keys":
                    pe.wait_ge(xhat, g + 1)
                    for t in range(CT):
                        for b in range(GB):
                            pe.matmul(KZ[:, t * GT + b * P:t * GT + (b + 1) * P], XHAT[:, b, t * P:(t + 1) * P], IDENT, is_transpose=True,
                                      start=(t == 0 and b == 0), stop=False, skip_group_check=True)
                        i = pe.matmul(KZ[:, t * GT:(t + 1) * GT], WPLUS[:, t * P:(t + 1) * P], STEPR[:, :], start=False, stop=True,
                                      skip_group_check=True)
                    i.then_inc(k_turned, 1)
                    pe.wait_ge(ctx_in, 16 * (g + 1))
                    for t in range(CT):
                        for b in range(GB):
                            i = pe.transpose(VX[:, t * GT + b * P:t * GT + (b + 1) * P], V[:, b, t * P:(t + 1) * P], IDENT)
                    i.then_inc(v_turned, 1)
                elif stage == "residual":
                    pe.wait_ge(y_ready, g + 1)
                    for b in range(GB):
                        for t in range(CT):
                            i = pe.transpose(YB[:, b * C + t * P:b * C + (t + 1) * P], Y[:, t, b, :], IDENT)
                    i.then_inc(y_turned, 1)
                elif stage == "turn":
                    pe.wait_ge(z_ready, g + 1)
                    for t in range(CT):
                        for b in range(GB):
                            i = pe.transpose(KZ[:, t * GT + b * P:t * GT + (b + 1) * P], Z[:, b, t * P:(t + 1) * P], IDENT)
                    i.then_inc(z_turned, 1)
                elif stage == "fwht":
                    pe.wait_ge(z_hi, g + 1)
                    for o in range(CT):
                        for n, part in enumerate((ZH, ZL)):
                            if n == 1 and o == 0:
                                pe.wait_ge(z_lo, g + 1)
                            for t in range(CT):
                                i = pe.matmul(VX[:, o * GT:(o + 1) * GT], (HN if o and t else HP)[:, :], part[:, t, :],
                                              start=(n == 0 and t == 0), stop=(n == 1 and t == CT - 1))
                    i.then_inc(f_full, 1)

            pe.wait_ge(const_in, 16)
            pe.wait_ge(vec_in, 16)
            pe.transpose(YB[:, 0:NV], VR[:, :], HI[0:NV, P:P + NV]).then_inc(vecs_turned, 1)
            pe.wait_ge(wplus, 4)
            front("keys", 0)

            def prep(n):
                if n >= NBANKS:
                    pe.wait_ge(bank_read, n - NBANKS + 1)
                m, j0 = divmod(2 * n, JT)
                if j0 == 0:
                    pe.wait_ge(wug_in[m], 16)
                for i in range(2):
                    for t in range(CT):
                        o = (i * CT + t) * P
                        a = pe.transpose(fill(n)[:, o:o + P], WN[:, m, j0 + i, t * P:(t + 1) * P], IDENT)
                a.then_inc(bank_full, 1)

            for n in range(4):
                prep(n)
            front("residual", 0)
            for n in range(4, UG_FILLS):
                prep(n)
            front("turn", 0)
            pe.wait_ge(consts_r, 2)
            front("fwht", 0)

            pe.wait_ge(fly_p, 6)
            pe.wait_ge(fly_v, 6)
            for n in range(DT_FILLS):
                m = UG_FILLS + n
                pe.wait_ge(bank_read, m - NBANKS + 1)
                for i in range(2):
                    for t in range(CT):
                        o = i * C + t * P
                        a = pe.transpose(fill(m)[:, o:o + P], DB[:, t, 2 * n + i, :], IDENT)
                a.then_inc(bank_full, 1)
            for n in range(DM_FILLS):
                m = UG_FILLS + DT_FILLS + n
                pe.wait_ge(bank_read, m - NBANKS + 1)
                for part in (DTH, DTL):
                    a = pe.matmul(fill(m)[:, :], HP[:, :], part[:, 2 * n:2 * n + 2, :].rearrange("p j c -> p (j c)"),
                                  start=(part is DTH), stop=(part is DTL))
                a.then_inc(bank_full, 1)

            def ffn(g, nxt):
                def up(j):
                    pe.wait_ge(bank_read, PREP + g * JT + j - NBANKS + 1)
                    for m in range(2):
                        n = 0
                        for t in range(CT):
                            for w, f in ((WTH, FH), (WTH, FL), (WTL, FH)):
                                a = pe.matmul(fill(j)[:, m * GT:(m + 1) * GT], w[:, m, j, t, :],
                                              f[:, bass.ds(g, 1), t, :].rearrange("p o n -> p (o n)"), start=(n == 0), stop=(n == 5))
                                n += 1
                    a.then_inc(bank_full, 1)

                def down(j):
                    pe.wait_ge(h_lo, g * JT + j + 1)
                    if j == 0:
                        pe.wait_ge(out_ready, g + 1)
                    for b in range(GB):
                        for n, (h, m) in enumerate(((HH, MH), (HH, ML), (HL, MH))):
                            a = pe.matmul(OD[:, b * C:(b + 1) * C], h[:, j, b * P:(b + 1) * P], m[:, j, :],
                                          start=(j == 0 and b == 0 and n == 0), stop=(j == JT - 1 and n == 2), skip_group_check=True)
                    if j == JT - 1:
                        a.then_inc(down_full, 1)

                pe.wait_ge(f_lo, g + 1)
                for j in range(JT):
                    up(j)
                    if j >= LAG:
                        down(j - LAG)
                    for stage in FRONT_SLOTS.get(j, []) if nxt is not None else []:
                        front(stage, nxt)
                for j in range(JT - LAG, JT):
                    down(j)

            pe.wait_ge(bank_read, PREP)
            with pe.Fori(0, NG - 1) as g:
                ffn(g, g + 1)
            ffn(NG - 1, None)


def hadamard(n):
    import numpy as np

    h = np.ones((1, 1), np.float32)
    while h.shape[0] < n:
        h = np.block([[h, h], [h, -h]])
    return h


def kernel(**inputs):
    import concourse.bacc as bacc
    import numpy as np
    from concourse.bass_utils import run_bass_kernel_spmd

    flat = ("L0_xattn_w", "L0_xattn_u", "L0_ffn_SU_ug", "L0_ffn_SU_dp", "L0_ffn_Wscale_ug", "L0_ffn_Wscale_dp")
    arrays = {
        "x": np.ascontiguousarray(inputs["x"]),
        "ctx": np.ascontiguousarray(inputs["ctx_2048"]),
        "vecs": np.concatenate([np.asarray(inputs[n]) for n in flat]).reshape(NV, P),
        "gates": np.ascontiguousarray(np.broadcast_to(np.concatenate([np.asarray(inputs["g_xattn"]), np.asarray(inputs["g_ffn"])]), (P, 2))),
        "consts": np.ascontiguousarray(np.concatenate([hadamard(P), np.eye(P, dtype=np.float32)], axis=1)),
        "steps": np.tile(np.arange(P, dtype=np.float32), GB).reshape(1, GT),
        "w_up": np.ascontiguousarray(inputs["L0_ffn_W_up"]),
        "w_gate": np.ascontiguousarray(inputs["L0_ffn_W_gate"]),
        "w_down": np.ascontiguousarray(inputs["L0_ffn_W_down"]),
    }
    nc = bacc.Bacc("TRN2", target_bir_lowering=False, num_devices=1)
    arrays = {f"in_{n}": a for n, a in arrays.items()}
    args = [nc.dram_tensor(n, a.shape, F32, kind="ExternalInput").ap() for n, a in arrays.items()]
    out = nc.dram_tensor("out_0", (NB, P, C), F32, kind="ExternalOutput").ap()
    build(nc, *args, out)
    return run_bass_kernel_spmd(nc, [arrays], core_ids=[0]).results[0]["out_0"]
```

```python
from contextlib import ExitStack

import concourse.bass as bass
from concourse import mybir

F32 = mybir.dt.float32
F32R = mybir.dt.float32r
ALU = mybir.AluOpType
ACT = mybir.ActivationFunctionType

P = 128
NB = 8
C = 256
INTER = 1024
CT = C // P
JT = INTER // P
GB = 2
NG = NB // GB
GT = GB * P
PAD = P + 1
SLOTS = NG * JT
EPS = 1e-5
C_MAX, C_MIN = 56.0, -50.0
M_NEG, M_POS = 0.45, 0.05
SCALE_UG = C ** -0.5
SCALE_DP = INTER ** -0.5

V_W, V_U, V_SUG, V_SDP, V_SUP, V_SGATE, V_SOUT = 0, 2, 4, 6, 14, 22, 30
NV = 32

NBANKS = 4
LAG = 5
RING = 4

PE_STAGES = {
    -1: [("keys", 0), ("values", 0), ("w", 2), ("w", 0), ("w_rest", 0), ("w", 3), ("w", 1), ("w_rest", 2), ("w_rest", 1), ("values", 1),
         ("y", 0), ("w", 4), ("w_rest", 3), ("w", 7), ("keys", 1), ("w_rest", 4), ("w", 5), ("w_rest", 7), ("turn", 0), ("w", 6),
         ("w_rest", 5), ("fwht", 0), ("w_rest", 6)], 0: [("d", 0), ("d", 1), ("d", 3), ("d", 2), ("m", 0), ("m", 1), ("m", 3), ("keys", 2),
         ("m", 2)], 3: [("values", 2)], 4: [("y", 1)], 6: [("turn", 1)], 7: [("fwht", 1), ("keys", 3)], 11: [("y", 2)], 13: [("turn", 2),
         ("values", 3)], 14: [("fwht", 2)], 16: [("y", 3)], 19: [("turn", 3)], 21: [("fwht", 3)]}
ACT_STAGES = {
    -1: [("setup", 0), ("keys", 0), ("w_hi", 2), ("w_hi", 0), ("recip", 0), ("w_hi", 1), ("w_lo", 0), ("w_lo", 1), ("w_lo", 2),
         ("w_hi", 3), ("w_hi", 4), ("w_lo", 3), ("w_hi", 7), ("keys", 1), ("silu_table", 0), ("turn", 0), ("w_hi", 5), ("w_lo", 4),
         ("w_lo", 5), ("w_lo", 7), ("fwht", 0), ("w_hi", 6), ("w_lo", 6)], 0: [("d_hi", 0), ("d_hi", 1), ("d_hi", 3), ("d_hi", 2),
         ("m_hi", 0), ("m_hi", 1), ("m_hi", 3), ("exp_block", (1, 2)), ("m_hi", 2)], 6: [("turn", 1)], 7: [("fwht", 1),
         ("exp_block", (2, 3))], 13: [("turn", 2), ("exp_block", (3, None))], 14: [("fwht", 2)], 19: [("turn", 3)], 21: [("fwht", 3)]}
DVE_STAGES = {
    -1: [("stats1", 0), ("setup_rows", 0), ("norm1", 0), ("setup_shift", 0), ("scan_a", 0), ("av", 0), ("mix_den", 0), ("scan_av", 0),
         ("mix_num", 0), ("estimate", 0), ("stats1", 1), ("newton", 0), ("fly", (1, 0)), ("norm1", 1), ("residual", 0), ("stats2", 0),
         ("fly", (1, 3)), ("norm2", 0), ("fly", (1, 4)), ("av", 1), ("scan_a", 1), ("turn", 0), ("scan_av", 1), ("mix_den", 1),
         ("fwht", 0), ("mix_num", 1), ("fly", (1, 5)), ("stats1", 2)], 0: [("d_lo", 0), ("d_lo", 1), ("d_lo", 3), ("norm1", 2),
         ("m_lo", 0), ("d_lo", 2), ("m_lo", 1), ("m_lo", 3), ("stats1", 3), ("norm1", 3), ("estimate", 1), ("m_lo", 2)],
    2: [("newton", 1)], 3: [("residual", 1), ("stats2", 1)], 5: [("norm2", 1), ("av", 2)], 6: [("scan_a", 2), ("turn", 1), ("mix_den", 2)],
    7: [("scan_av", 2), ("fwht", 1), ("mix_num", 2), ("estimate", 2)], 9: [("newton", 2)], 10: [("scan_a", 3), ("residual", 2),
         ("stats2", 2)], 12: [("norm2", 2)], 13: [("mix_den", 3), ("turn", 2), ("av", 3), ("scan_av", 3), ("mix_num", 3), ("estimate", 3)],
    14: [("fwht", 2)], 15: [("newton", 3)], 16: [("residual", 3), ("stats2", 3)], 17: [("norm2", 3)], 19: [("turn", 3)], 21: [("fwht", 3)]}
POOL_STAGES = {
    -1: [("rstd1", 0), ("setup", 0), ("scale", 0), ("fly", (0, 1)), ("error", 0), ("scale", 1), ("rstd1", 1), ("fly", (1, 1)),
         ("fly", (1, 2)), ("rstd2", 0), ("fly", (0, 0)), ("fly", (0, 2)), ("fly", (0, 3)), ("fly", (0, 4)), ("fly", (0, 5)), ("rstd1", 2),
         ("rstd1", 3), ("error", 1)], 3: [("rstd2", 1)], 6: [("error", 2)], 10: [("rstd2", 2)], 12: [("error", 3)], 15: [("rstd2", 3)]}


def stages(table):
    return [item for q in range(-1, SLOTS) for item in table.get(q, [])]


ORDER = []
for q in range(-1, SLOTS):
    if q >= 0:
        ORDER.append(("up", q))
    ORDER += [item for item in PE_STAGES.get(q, []) if item[0] in ("w", "d", "m")]
INDEX = {item: n for n, item in enumerate(ORDER)}
KZ_FILLS = [item for item in stages(PE_STAGES) if item[0] in ("keys", "turn")]
VX_FILLS = [item for item in stages(PE_STAGES) if item[0] in ("values", "fwht")]
HI_ON_ACT = [(name[0], n) for name, n in stages(ACT_STAGES) if name.endswith("_hi")]
LO_ON_ACT = [(name[0], n) for name, n in stages(ACT_STAGES) if name.endswith("_lo")]
RESTS = [(name[0], n) for name, n in stages(PE_STAGES) if name.endswith("_rest")]
LO_ON_DVE = [(name[0], n) for name, n in stages(DVE_STAGES) if name.endswith("_lo")]


def build(nc, x, ctx, vecs, consts, steps, w_up, w_gate, w_down, out):
    with ExitStack() as stack:
        def sb(name, shape, dt=F32):
            return stack.enter_context(nc.sbuf_tensor(name, shape, dt))

        def bank(name):
            return stack.enter_context(nc.psum_tensor(name, [P, 512], F32))

        def sem(name):
            return stack.enter_context(nc.semaphore(name))

        X = sb("X", [P, NB, C])
        V = sb("V", [P, NB, C])
        VR = sb("VR", [NV, P])
        VT = sb("VT", [P, NV])
        TG = sb("TG", [P, 2])
        HI = sb("HI", [P, 2 * P + 2])
        HP = sb("HP", [P, P], F32R)
        HN = sb("HN", [P, P], F32R)
        NI = sb("NI", [P, P], F32R)
        STEP = sb("STEP", [P, CT, GT])
        STEPR = sb("STEPR", [P, CT, GT], F32R)
        NEGW = sb("NEGW", [CT, P])
        WPLUS = sb("WPLUS", [P, P], F32R)
        DEC = sb("DEC", [P, CT])
        NHALF = sb("NHALF", [P, GB])
        SUMU = sb("SUMU", [P, CT])
        CUR = sb("CUR", [P, CT])
        RATIO = sb("RATIO", [P, CT])
        MPOS = sb("MPOS", [P, CT])
        NEGM = sb("NEGM", [P, CT])
        D = sb("D", [P, CT, GB, PAD])
        ALPHA = sb("ALPHA", [P, JT])
        OUTS = sb("OUTS", [P, CT])
        WN = sb("WN", [P, 2, JT, C])
        WTH = sb("WTH", [P, 2, JT, CT, P], F32R)
        WTL = sb("WTL", [P, 2, JT, CT, P], F32R)
        DN = sb("DN", [P, CT, JT, P])
        DB = sb("DB", [P, CT, JT, P])
        DTH = sb("DTH", [P, JT, C], F32R)
        DTL = sb("DTL", [P, JT, C], F32R)
        MH = sb("MH", [P, JT, C], F32R)
        ML = sb("ML", [P, JT, C], F32R)
        BS1, BS2 = (sb(n, [P, GB, 6]) for n in ("BS1", "BS2"))
        MV1, MV2 = (sb(n, [P, GB, 2]) for n in ("MV1", "MV2"))
        VE1, VE2, RS1, RS2 = (sb(n, [P, GB]) for n in ("VE1", "VE2", "RS1", "RS2"))
        XHAT = sb("XHAT", [P, GB, C])
        Z = sb("Z", [P, GB, C])
        EA = sb("EA", [P, NG, CT, GB, PAD])
        EV = sb("EV", [P, NG, CT, GB, PAD])
        SQ = sb("SQ", [P, CT, GB, PAD])
        SP_ = sb("SP_", [P, CT, GB, PAD])
        NUM, DEN, LND, R0, ERR, Y0, Y = (sb(n, [P, CT, GB, P]) for n in ("NUM", "DEN", "LND", "R0", "ERR", "Y0", "Y"))
        ZH = sb("ZH", [P, CT, GT], F32R)
        ZL = sb("ZL", [P, CT, GT], F32R)
        FH = sb("FH", [P, 2, CT, GT], F32R)
        FL = sb("FL", [P, 2, CT, GT], F32R)
        S = sb("S", [P, RING, GT])
        H = sb("H", [P, RING, GT])
        HH = sb("HH", [P, JT, GT], F32R)
        HL = sb("HL", [P, JT, GT], F32R)

        UG = [bank(f"UG{i}") for i in range(NBANKS)]
        OD = bank("OD")
        KZ = bank("KZ")
        VX = bank("VX")
        YB = bank("YB")
        IDENT = HI[:, P:2 * P]

        x_in = [sem(f"x{i}_in") for i in range(3)]
        ctx_in = [sem(f"ctx{i}_in") for i in range(3)]
        const_in, vec_in, step_in, stored = (sem(n) for n in ("const_in", "vec_in", "step_in", "stored"))
        w_in = {(m, h): sem(f"w{m}{h}_in") for m in range(2) for h in range(2)}
        wd_in = [sem(f"wd{t}_in") for t in range(CT)]
        step_clear, plus_clear, pads, d_clear, half = (sem(n) for n in ("step_clear", "plus_clear", "pads", "d_clear", "half"))
        vecs_turned, vecs_kept, tanh_gate, decay_ready, c_ready, m_ready, ratio_ready, decay_set = (sem(n) for n in (
            "vecs_turned", "vecs_kept", "tanh_gate", "decay_ready", "c_ready", "m_ready", "ratio_ready", "decay_set"))
        consts_r, wplus, steps_r, alpha, outs = (sem(n) for n in ("consts_r", "wplus", "steps_r", "alpha", "outs"))
        bank_full, rest_full = sem("bank_full"), sem("rest_full")
        bank_hi, lo_on_act, bank_read = sem("bank_hi"), sem("lo_on_act"), sem("bank_read")
        wd_scaled = [sem(f"wd{t}_scaled") for t in range(CT)]
        flown = [sem(f"flown{t}") for t in range(CT)]
        stats1, mv1, ve1, rstd1, xhat, k_turned, v_turned, a_ready, av_ready = (sem(n) for n in (
            "stats1", "mv1", "ve1", "rstd1", "xhat", "k_turned", "v_turned", "a_ready", "av_ready"))
        scanned, mixed, ln_ready, r0_ready, err_ready, y0_ready, y_ready, y_turned = (sem(n) for n in (
            "scanned", "mixed", "ln_ready", "r0_ready", "err_ready", "y0_ready", "y_ready", "y_turned"))
        x1_ready, stats2, mv2, ve2, rstd2, z_ready, z_turned, z_hi, z_lo, f_full, f_hi, f_lo = (sem(n) for n in (
            "x1_ready", "stats2", "mv2", "ve2", "rstd2", "z_ready", "z_turned", "z_hi", "z_lo", "f_full", "f_hi", "f_lo"))
        silu_ready, h_ready, h_hi, h_lo, down_full, out_ready = (sem(n) for n in (
            "silu_ready", "h_ready", "h_hi", "h_lo", "down_full", "out_ready"))

        x_v = x.rearrange("b p c -> p b c")
        ctx_v = ctx.rearrange("b p c -> p b c")
        out_v = out.rearrange("b p c -> p b c")

        def total(g, b):
            last = g == NG - 1 and b == GB - 1
            return (VX if last else OD)[:, (0 if last else b * C):(C if last else (b + 1) * C)]

        def fill(item):
            return UG[INDEX[item] % NBANKS]

        def wait_lo(eng, item):
            if item in LO_ON_ACT:
                eng.wait_ge(lo_on_act, LO_ON_ACT.index(item) + 1)
            else:
                eng.wait_ge(bank_read, LO_ON_DVE.index(item) + 1)

        def wait_bank_free(eng, item):
            n = INDEX[item] - NBANKS
            if n >= 0:
                last = ORDER[n]
                if last[0] == "up":
                    eng.wait_ge(h_ready, last[1] + 1)
                else:
                    wait_lo(eng, last)

        def n_hi(item):
            return HI_ON_ACT.index(item) + 1

        def parts(item):
            kind, n = item
            if kind == "w":
                m, j = n % 2, 2 * (n // 2)
                return [t[:, m, j:j + 2, :, :].rearrange("p j t q -> p (j t q)") for t in (WTH, WTL)]
            return [t[:, 2 * n:2 * n + 2, :].rearrange("p j c -> p (j c)") for t in ((DTH, DTL) if kind == "d" else (MH, ML))]

        def fly(eng, t, n):
            step = n // 2
            src, dst = (DN, DB) if step % 2 == 0 else (DB, DN)
            s, d = (a[:, t, :, :].rearrange("p (n two h) q -> p n two (h q)", two=2, h=1 << step) for a in (src, dst))
            if step == 0:
                eng.wait_ge(wd_scaled[t], 1)
            else:
                eng.wait_ge(flown[t], 2 * step)
            eng.tensor_tensor(d[:, :, n % 2, :], s[:, :, 0, :], s[:, :, 1, :], ALU.subtract if n % 2 else ALU.add).then_inc(flown[t], 1)

        def arrival(g):
            return min(g, 2)

        block = stack.enter_context(nc.Block())

        @block.sync
        def _(sp):
            def load_x(i):
                b = slice(GB * i, GB * (i + 1) if i < 2 else NB)
                sp.dma_start(X[:, b, :], x_v[:, b, :]).then_inc(x_in[i], 16)

            def load_ctx(i):
                b = slice(GB * i, GB * (i + 1) if i < 2 else NB)
                sp.dma_start(V[:, b, :], ctx_v[:, b, :]).then_inc(ctx_in[i], 16)

            load_x(0)
            sp.dma_start(VR[:, :], vecs).then_inc(vec_in, 16)
            sp.dma_start(HI[:, :], consts).then_inc(const_in, 16)
            sp.wait_ge(step_clear, 1)
            sp.dma_start(STEP[0:32 + CT, :, :].rearrange("p t n -> p (t n)"), steps).then_inc(step_in, 16)
            load_ctx(0)
            def load_w(m, h):
                j = slice(h * JT // 2, (h + 1) * JT // 2)
                sp.dma_start(WN[:, m, j, :], (w_gate, w_up)[m].rearrange("(t p) c -> p t c", p=P)[:, j, :]).then_inc(w_in[m, h], 16)

            def load_down(t):
                sp.dma_start(DN[:, t, :, :], w_down.rearrange("(t p) (j q) -> p t j q", p=P, q=P)[:, t, :, :]).then_inc(wd_in[t], 16)

            load_w(0, 0)
            load_down(0)
            load_w(1, 0)
            load_down(1)
            load_x(1)
            load_ctx(1)
            load_w(0, 1)
            load_w(1, 1)
            load_x(2)
            load_ctx(2)
            leaving = [slice(GB * g, GB * (g + 1)) for g in range(NG - 1)] + [slice(b, b + 1) for b in range(NB - GB, NB)]
            for n, b in enumerate(leaving):
                sp.wait_ge(out_ready, n + 1)
                sp.dma_start(out_v[:, b, :], X[:, b, :]).then_inc(stored, 16)
            sp.wait_ge(stored, 16 * len(leaving))

        @block.gpsimd
        def _(pool):
            pool.memset(STEP[:, :, :], 0.0).then_inc(step_clear, 1)
            pool.memset(WPLUS[:, :].bitcast(F32), 0.0).then_inc(plus_clear, 1)
            pool.memset(NHALF[:, :], -0.5).then_inc(half, 1)
            pool.memset(D[:, :, :, :], 0.0).then_inc(d_clear, 1)
            pool.memset(EA[:, :, :, :, 0:1], 0.0).then_inc(pads, 1)
            pool.memset(EV[:, :, :, :, 0:1], 0.0).then_inc(pads, 1)

            def stage(name, g):
                if name == "setup":
                    pool.wait_ge(d_clear, 1)
                    pool.wait_ge(decay_ready, 2)
                    for t in range(CT):
                        pool.tensor_scalar(D[:, t, :, 1:PAD], D[:, t, :, 1:PAD], 1.0, DEC[:, t:t + 1], ALU.mult, ALU.add).then_inc(decay_set, 1)
                    pool.wait_ge(tanh_gate, 2)
                    pool.tensor_scalar(OUTS[:, :], VT[:, V_SOUT:V_SOUT + CT], TG[:, 1:2], 1.0, ALU.mult, ALU.mult).then_inc(outs, 1)
                    pool.tensor_scalar(ALPHA[:, :], VT[:, V_SUP:V_SUP + JT], SCALE_DP, 1.0, ALU.mult, ALU.mult).then_inc(alpha, 1)
                    pool.wait_ge(alpha, 1)
                    pool.tensor_tensor(ALPHA[:, :], ALPHA[:, :], VT[:, V_SDP:V_SDP + JT], ALU.mult).then_inc(alpha, 1)
                elif name in ("rstd1", "rstd2"):
                    ve, VE, rstd, RS = (ve1, VE1, rstd1, RS1) if name == "rstd1" else (ve2, VE2, rstd2, RS2)
                    pool.wait_ge(half, 1)
                    pool.wait_ge(ve, g + 1)
                    pool.tensor_tensor(RS[:, :], VE[:, :], NHALF[:, :], ALU.pow).then_inc(rstd, 1)
                elif name == "error":
                    pool.wait_ge(r0_ready, g + 1)
                    pool.tensor_tensor(ERR[:, :, :, :], DEN[:, :, :, :], R0[:, :, :, :], ALU.mult).then_inc(err_ready, 1)
                elif name == "scale":
                    pool.wait_ge(outs, 1)
                    pool.wait_ge(wd_in[g], 16)
                    pool.tensor_scalar(DN[:, g, :, :], DN[:, g, :, :], OUTS[:, g:g + 1], 1.0, ALU.mult, ALU.mult).then_inc(wd_scaled[g], 1)
                elif name == "fly":
                    fly(pool, *g)

            for q in range(-1, SLOTS):
                if q >= 0:
                    pool.wait_ge(h_hi, q + 1)
                    pool.tensor_tensor(HL[:, q % JT, :], H[:, q % RING, :], HH[:, q % JT, :].bitcast(F32), ALU.subtract).then_inc(h_lo, 1)
                for name, g in POOL_STAGES.get(q, []):
                    stage(name, g)

        @block.scalar
        def _(act):
            def keys(g):
                act.wait_ge(k_turned, g + 1)
                if g == 0:
                    act.wait_ge(m_ready, 2)
                    act.wait_ge(pads, 1)
                for t in range(CT):
                    i = act.activation(EA[:, g, t, :, 1:PAD], KZ[:, t * GT:(t + 1) * GT].rearrange("p (b q) -> p b q", b=GB),
                                       ACT.Exp, bias=NEGM[:, t:t + 1])
                i.then_inc(a_ready, 1)

            def reciprocal(g):
                act.wait_ge(mixed, 2 * g + 1)
                act.activation(LND[:, :, :, :], DEN[:, :, :, :], ACT.Ln).then_inc(ln_ready, 1)
                act.wait_ge(ln_ready, g + 1)
                act.activation(R0[:, :, :, :], LND[:, :, :, :], ACT.Exp, scale=-1.0).then_inc(r0_ready, 1)

            def stage(name, g):
                if name == "setup":
                    act.preload_act_table_set("exp_and_others")
                    act.wait_ge(const_in, 16)
                    act.activation(TG[:, 0:1], HI[:, 2 * P:2 * P + 1], ACT.Tanh, scale=-1.0).then_inc(tanh_gate, 1)
                    act.activation(TG[:, 1:2], HI[:, 2 * P + 1:2 * P + 2], ACT.Tanh).then_inc(tanh_gate, 1)
                    act.preload_act_table_set("natural_log_exp_and_others")
                    act.activation(HP[:, :], HI[:, 0:P], ACT.Copy).then_inc(consts_r, 1)
                    act.activation(HN[:, :], HI[:, 0:P], ACT.Copy, scale=-1.0).then_inc(consts_r, 1)
                    act.activation(NI[:, :], IDENT, ACT.Copy, scale=-1.0).then_inc(consts_r, 1)
                    act.wait_ge(step_in, 16)
                    act.activation(STEPR[:, :, :], STEP[:, :, :], ACT.Copy).then_inc(steps_r, 1)
                    act.wait_ge(decay_ready, 1)
                    act.activation(DEC[:, :], DEC[:, :], ACT.Exp).then_inc(decay_ready, 1)
                    act.wait_ge(c_ready, 3)
                    act.activation(RATIO[:, :], CUR[:, :], ACT.Exp).then_inc(ratio_ready, 1)
                elif name == "keys":
                    keys(g)
                elif name == "recip":
                    reciprocal(g)
                elif name == "silu_table":
                    act.preload_act_table_set("silu_and_others")
                elif name == "exp_block":
                    act.preload_act_table_set("natural_log_exp_and_others")
                    reciprocal(g[0])
                    if g[1] is not None:
                        keys(g[1])
                    act.preload_act_table_set("silu_and_others")
                elif name == "scale":
                    act.wait_ge(outs, 1)
                    act.wait_ge(wd_in[g], 16)
                    act.activation(DN[:, g, :, :], DN[:, g, :, :], ACT.Copy, scale=OUTS[:, g:g + 1]).then_inc(wd_scaled[g], 1)
                elif name.endswith("_hi"):
                    item = (name[0], g)
                    act.wait_ge(bank_full, INDEX[item] + 1)
                    act.activation(parts(item)[0], fill(item)[:, :], ACT.Copy).then_inc(bank_hi, 1)
                elif name.endswith("_lo"):
                    item = (name[0], g)
                    act.wait_ge(rest_full, RESTS.index(item) + 1)
                    act.activation(parts(item)[1], fill(item)[:, :], ACT.Copy).then_inc(lo_on_act, 1)
                elif name == "turn":
                    act.wait_ge(z_turned, g + 1)
                    for t in range(CT):
                        act.activation(ZH[:, t, :], KZ[:, t * GT:(t + 1) * GT], ACT.Copy, scale=VT[:, V_SUG + t:V_SUG + t + 1]).then_inc(z_hi, 1)
                elif name == "fwht":
                    act.wait_ge(f_full, g + 1)
                    act.activation(FH[:, g % 2, :, :], VX[:, :].rearrange("p (t n) -> p t n", t=CT), ACT.Copy, scale=SCALE_UG).then_inc(f_hi, 1)

            def hi(q):
                act.wait_ge(h_ready, q + 1)
                act.activation(HH[:, q % JT, :], H[:, q % RING, :], ACT.Copy).then_inc(h_hi, 1)

            def gate(q):
                j = q % JT
                act.wait_ge(bank_full, INDEX["up", q] + 1)
                act.activation(S[:, q % RING, :], fill(("up", q))[:, 0:GT], ACT.Silu, scale=VT[:, V_SGATE + j:V_SGATE + j + 1]).then_inc(silu_ready, 1)
                if q:
                    hi(q - 1)

            for q in range(-1, SLOTS):
                if q >= 0:
                    gate(q)
                for name, g in ACT_STAGES.get(q, []):
                    stage(name, g)
            hi(SLOTS - 1)

        @block.vector
        def _(dve):
            def statistics(g, BS, stats, MV, mv, VE, ve):
                for b in range(GB):
                    dve.bn_stats(BS[:, b, :], X[:, GB * g + b, :]).then_inc(stats, 1)
                dve.wait_ge(stats, (g + 1) * GB)
                for b in range(GB):
                    i = dve.bn_aggr(MV[:, b, :], BS[:, b, :])
                i.then_inc(mv, 1)
                dve.wait_ge(mv, g + 1)
                dve.tensor_scalar(VE[:, :], MV[:, :, 1], EPS, None, ALU.add).then_inc(ve, 1)

            def normalise(g, dst, MV, RS, rstd, ready):
                dve.wait_ge(rstd, g + 1)
                for b in range(GB):
                    i = dve.tensor_scalar(dst[:, b, :], X[:, GB * g + b, :], MV[:, b, 0:1], RS[:, b:b + 1], ALU.subtract, ALU.mult)
                i.then_inc(ready, 1)

            def stage(name, g):
                if name == "stats1":
                    dve.wait_ge(x_in[arrival(g)], 16)
                    if g:
                        dve.wait_ge(xhat, g)
                    statistics(g, BS1, stats1, MV1, mv1, VE1, ve1)
                elif name == "norm1":
                    if g:
                        dve.wait_ge(k_turned, g)
                    normalise(g, XHAT, MV1, RS1, rstd1, xhat)
                elif name == "av":
                    if g == 0:
                        dve.wait_ge(pads, 2)
                    dve.wait_ge(v_turned, g + 1)
                    dve.wait_ge(a_ready, g + 1)
                    dve.tensor_tensor(EV[:, g, :, :, 1:PAD].rearrange("p t b q -> p (t b) q"), EA[:, g, :, :, 1:PAD].rearrange("p t b q -> p (t b) q"),
                                      VX[:, :].rearrange("p (n q) -> p n q", q=P), ALU.mult).then_inc(av_ready, 1)
                elif name in ("scan_a", "scan_av"):
                    n, ready, src, dst = (0, a_ready, EA, SQ) if name == "scan_a" else (1, av_ready, EV, SP_)
                    if g == 0:
                        dve.wait_ge(decay_set, 2)
                    else:
                        dve.wait_ge(mixed, 2 * g - 1 + n)
                    dve.wait_ge(ready, g + 1)
                    flat = "p t b q -> p (t b q)"
                    dve.tensor_tensor_scan(dst[:, :, :, :].rearrange(flat), D[:, :, :, :].rearrange(flat), src[:, g, :, :, :].rearrange(flat),
                                           0.0, ALU.mult, ALU.add).then_inc(scanned, 1)
                elif name in ("mix_den", "mix_num"):
                    n, dst, cur, state = (0, DEN, EA, SQ) if name == "mix_den" else (1, NUM, EV, SP_)
                    if g == 0:
                        dve.wait_ge(ratio_ready, 1)
                    else:
                        dve.wait_ge(y_ready, g)
                    dve.wait_ge(scanned, 2 * g + n + 1)
                    for t in range(CT):
                        i = dve.scalar_tensor_tensor(out=dst[:, t, :, :], in0=cur[:, g, t, :, 1:PAD], scalar=RATIO[:, t:t + 1],
                                                     in1=state[:, t, :, 0:P], op0=ALU.mult, op1=ALU.add)
                    i.then_inc(mixed, 1)
                elif name == "estimate":
                    dve.wait_ge(r0_ready, g + 1)
                    dve.wait_ge(mixed, 2 * g + 2)
                    dve.tensor_tensor(Y0[:, :, :, :], NUM[:, :, :, :], R0[:, :, :, :], ALU.mult).then_inc(y0_ready, 1)
                elif name == "newton":
                    dve.wait_ge(err_ready, g + 1)
                    dve.wait_ge(y0_ready, g + 1)
                    dve.scalar_tensor_tensor(out=Y[:, :, :, :].rearrange("p t b q -> p (t b q)"), in0=ERR[:, :, :, :].rearrange("p t b q -> p (t b q)"),
                                             scalar=2.0, in1=Y0[:, :, :, :].rearrange("p t b q -> p (t b q)"), op0=ALU.subtract,
                                             op1=ALU.mult).then_inc(y_ready, 1)
                elif name == "residual":
                    dve.wait_ge(y_turned, g + 1)
                    xg = X[:, GB * g:GB * (g + 1), :]
                    dve.scalar_tensor_tensor(out=xg, in0=YB[:, :].rearrange("p (b c) -> p b c", b=GB), scalar=TG[:, 0:1], in1=xg,
                                             op0=ALU.mult, op1=ALU.add).then_inc(x1_ready, 1)
                elif name == "stats2":
                    if g:
                        dve.wait_ge(z_ready, g)
                    dve.wait_ge(x1_ready, g + 1)
                    statistics(g, BS2, stats2, MV2, mv2, VE2, ve2)
                elif name == "norm2":
                    normalise(g, Z, MV2, RS2, rstd2, z_ready)
                elif name == "turn":
                    dve.wait_ge(z_hi, CT * (g + 1))
                    for t in range(CT):
                        i = dve.scalar_tensor_tensor(out=ZL[:, t, :], in0=KZ[:, t * GT:(t + 1) * GT], scalar=VT[:, V_SUG + t:V_SUG + t + 1],
                                                     in1=ZH[:, t, :].bitcast(F32), op0=ALU.mult, op1=ALU.subtract)
                    i.then_inc(z_lo, 1)
                elif name == "fwht":
                    dve.wait_ge(f_hi, g + 1)
                    dve.scalar_tensor_tensor(out=FL[:, g % 2, :, :].rearrange("p t n -> p (t n)"), in0=VX[:, :], scalar=SCALE_UG,
                                             in1=FH[:, g % 2, :, :].rearrange("p t n -> p (t n)").bitcast(F32),
                                             op0=ALU.mult, op1=ALU.subtract).then_inc(f_lo, 1)
                elif name == "scale":
                    dve.wait_ge(outs, 1)
                    dve.wait_ge(wd_in[g], 16)
                    dve.tensor_scalar(DN[:, g, :, :], DN[:, g, :, :], OUTS[:, g:g + 1], None, ALU.mult).then_inc(wd_scaled[g], 1)
                elif name == "fly":
                    fly(dve, *g)
                elif name.endswith("_lo"):
                    item = (name[0], g)
                    dve.wait_ge(bank_hi, n_hi(item))
                    hi, lo = parts(item)
                    dve.tensor_tensor(lo, fill(item)[:, :], hi.bitcast(F32), ALU.subtract).then_inc(bank_read, 1)

            def setup_rows():
                dve.wait_ge(vecs_turned, 1)
                dve.tensor_copy(VT[:, :], YB[:, 0:NV]).then_inc(vecs_kept, 1)
                dve.wait_ge(vec_in, 16)
                dve.tensor_scalar(NEGW[:, :], VR[V_W:V_W + CT, :], 0.0, -1.0, ALU.max, ALU.mult).then_inc(wplus, 1)
                dve.wait_ge(wplus, 1)
                dve.wait_ge(plus_clear, 1)
                dve.tensor_copy(WPLUS[0:CT, :], NEGW[:, :]).then_inc(wplus, 1)
                dve.wait_ge(vecs_kept, 1)
                dve.tensor_scalar(DEC[:, :], VT[:, V_W:V_W + CT], 0.0, None, ALU.min).then_inc(decay_ready, 1)
                dve.wait_ge(wplus, 2)
                dve.tensor_tensor(WPLUS[32:32 + CT, :], NEGW[:, :], WPLUS[0:CT, :].bitcast(F32), ALU.subtract).then_inc(wplus, 1)

            def setup_shift():
                dve.tensor_scalar(SUMU[:, :], VT[:, V_W:V_W + CT], 0.0, None, ALU.max).then_inc(c_ready, 1)
                dve.wait_ge(c_ready, 1)
                dve.tensor_tensor(SUMU[:, :], SUMU[:, :], VT[:, V_U:V_U + CT], ALU.add).then_inc(c_ready, 1)
                dve.wait_ge(c_ready, 2)
                dve.tensor_scalar(CUR[:, :], SUMU[:, :], C_MAX, C_MIN, ALU.min, ALU.max).then_inc(c_ready, 1)
                dve.wait_ge(c_ready, 3)
                dve.tensor_scalar(MPOS[:, :], CUR[:, :], 0.0, -M_POS, ALU.max, ALU.mult).then_inc(m_ready, 1)
                dve.wait_ge(m_ready, 1)
                dve.scalar_tensor_tensor(out=NEGM[:, :], in0=CUR[:, :], scalar=-M_NEG, in1=MPOS[:, :], op0=ALU.mult, op1=ALU.add).then_inc(m_ready, 1)

            def out(g):
                dve.wait_ge(down_full, g + 1)
                xg = X[:, GB * g:GB * (g + 1), :]
                dve.tensor_tensor(xg, OD[:, :].rearrange("p (b c) -> p b c", b=GB), xg, ALU.add).then_inc(out_ready, 1)

            def hidden(q):
                j = q % JT
                dve.wait_ge(silu_ready, q + 1)
                if q == 0:
                    dve.wait_ge(alpha, 2)
                if q >= RING:
                    dve.wait_ge(h_lo, q - RING + 1)
                dve.scalar_tensor_tensor(out=H[:, q % RING, :], in0=S[:, q % RING, :], scalar=ALPHA[:, j:j + 1], in1=fill(("up", q))[:, GT:2 * GT],
                                         op0=ALU.mult, op1=ALU.mult).then_inc(h_ready, 1)

            for q in range(-1, SLOTS):
                if q >= JT + LAG and (q - LAG) % JT == 0:
                    out((q - LAG) // JT - 1)
                if q >= 0:
                    hidden(q)
                for name, g in DVE_STAGES.get(q, []):
                    if name == "setup_rows":
                        setup_rows()
                    elif name == "setup_shift":
                        setup_shift()
                    else:
                        stage(name, g)
            for b in range(GB):
                dve.wait_ge(down_full, NG + b)
                xb = X[:, GB * (NG - 1) + b, :]
                dve.tensor_tensor(xb, total(NG - 1, b), xb, ALU.add).then_inc(out_ready, 1)

        @block.tensor
        def _(pe):
            def wait_read(item, fills):
                n = fills.index(item)
                if n:
                    name, g = fills[n - 1]
                    pe.wait_ge({"keys": a_ready, "turn": z_lo, "values": av_ready, "fwht": f_lo}[name], g + 1)

            def stage(name, g):
                if name == "keys":
                    wait_read(("keys", g), KZ_FILLS)
                    pe.wait_ge(xhat, g + 1)
                    for t in range(CT):
                        for b in range(GB):
                            pe.matmul(KZ[:, t * GT + b * P:t * GT + (b + 1) * P], XHAT[:, b, t * P:(t + 1) * P], IDENT, is_transpose=True,
                                      start=(t == 0 and b == 0), stop=False, skip_group_check=True)
                    if g == 0:
                        pe.wait_ge(wplus, 3)
                        pe.wait_ge(steps_r, 1)
                    for t in range(CT):
                        i = pe.matmul(KZ[:, t * GT:(t + 1) * GT], WPLUS[:, :], STEPR[:, t, :], start=False, stop=True, skip_group_check=True)
                    i.then_inc(k_turned, 1)
                elif name == "values":
                    pe.wait_ge(ctx_in[arrival(g)], 16)
                    wait_read(("values", g), VX_FILLS)
                    for t in range(CT):
                        for b in range(GB):
                            i = pe.transpose(VX[:, t * GT + b * P:t * GT + (b + 1) * P], V[:, GB * g + b, t * P:(t + 1) * P], IDENT)
                    i.then_inc(v_turned, 1)
                elif name == "y":
                    pe.wait_ge(y_ready, g + 1)
                    for b in range(GB):
                        for t in range(CT):
                            i = pe.transpose(YB[:, b * C + t * P:b * C + (t + 1) * P], Y[:, t, b, :], IDENT)
                    i.then_inc(y_turned, 1)
                elif name == "turn":
                    wait_read(("turn", g), KZ_FILLS)
                    pe.wait_ge(z_ready, g + 1)
                    for t in range(CT):
                        for b in range(GB):
                            i = pe.transpose(KZ[:, t * GT + b * P:t * GT + (b + 1) * P], Z[:, b, t * P:(t + 1) * P], IDENT)
                    i.then_inc(z_turned, 1)
                elif name == "fwht":
                    wait_read(("fwht", g), VX_FILLS)
                    pe.wait_ge(consts_r, 2)
                    for o in range(CT):
                        for n, part in enumerate((ZH, ZL)):
                            if n == 1 and o == 0:
                                pe.wait_ge(z_lo, g + 1)
                            for t in range(CT):
                                if n == 0 and o == 0:
                                    pe.wait_ge(z_hi, CT * g + t + 1)
                                i = pe.matmul(VX[:, o * GT:(o + 1) * GT], (HN if o and t else HP)[:, :], part[:, t, :],
                                              start=(n == 0 and t == 0), stop=(n == 1 and t == CT - 1))
                    i.then_inc(f_full, 1)

            def prep(item):
                kind, n = item
                wait_bank_free(pe, item)
                if kind == "m":
                    pe.wait_ge(consts_r, 1)
                    wait_lo(pe, ("d", n))
                    for h, part in enumerate((DTH, DTL)):
                        i = pe.matmul(fill(item)[:, :], HP[:, :], part[:, 2 * n:2 * n + 2, :].rearrange("p j c -> p (j c)"), start=(h == 0), stop=(h == 1))
                    i.then_inc(bank_full, 1)
                    return
                m, j0 = n % 2, 2 * (n // 2)
                if kind == "w":
                    pe.wait_ge(w_in[m, j0 // (JT // 2)], 16)
                else:
                    for t in range(CT):
                        pe.wait_ge(flown[t], 6)
                for i in range(2):
                    for t in range(CT):
                        o = (i * CT + t) * P
                        src = WN[:, m, j0 + i, t * P:(t + 1) * P] if kind == "w" else DB[:, t, 2 * n + i, :]
                        a = pe.transpose(fill(item)[:, o:o + P], src, IDENT) if item not in LO_ON_ACT else pe.matmul(
                            fill(item)[:, o:o + P], src, IDENT, is_transpose=True, start=(o == 0), stop=False, skip_group_check=True)
                a.then_inc(bank_full, 1)

            def take_hi_off(item):
                pe.wait_ge(bank_hi, n_hi(item))
                pe.wait_ge(consts_r, 3)
                pe.matmul(fill(item)[:, :], NI[:, :], parts(item)[0], start=False, stop=True, skip_group_check=True).then_inc(rest_full, 1)

            def up(q):
                g, j = divmod(q, JT)
                if j == 0:
                    pe.wait_ge(f_lo, g + 1)
                if q < JT and j % 2 == 0:
                    wait_lo(pe, ("w", j))
                    wait_lo(pe, ("w", j + 1))
                wait_bank_free(pe, ("up", q))
                for m in range(2):
                    n = 0
                    for t in range(CT):
                        for w, f in ((WTH, FH), (WTH, FL), (WTL, FH)):
                            a = pe.matmul(fill(("up", q))[:, m * GT:(m + 1) * GT], w[:, m, j, t, :], f[:, g % 2, t, :], start=(n == 0), stop=(n == 5))
                            n += 1
                a.then_inc(bank_full, 1)

            def down(q):
                g, j = divmod(q, JT)
                pe.wait_ge(h_lo, q + 1)
                if j == 0 and g:
                    pe.wait_ge(out_ready, g)
                if q < JT and j % 2 == 0:
                    wait_lo(pe, ("m", j // 2))
                for b in range(GB):
                    for n, (h, m) in enumerate(((HH, MH), (HH, ML), (HL, MH))):
                        a = pe.matmul(total(g, b), h[:, j, b * P:(b + 1) * P], m[:, j, :],
                                      start=(j == 0 and n == 0 and (b == 0 or g == NG - 1)), stop=(j == JT - 1 and n == 2), skip_group_check=True)
                    if j == JT - 1 and (b == GB - 1 or g == NG - 1):
                        a.then_inc(down_full, 1)

            pe.wait_ge(const_in, 16)
            pe.wait_ge(vec_in, 16)
            pe.transpose(YB[:, 0:NV], VR[:, :], HI[0:NV, P:P + NV]).then_inc(vecs_turned, 1)
            for q in range(-1, SLOTS):
                if q >= 0:
                    up(q)
                for name, g in PE_STAGES.get(q, []):
                    if name == "w_rest":
                        take_hi_off(("w", g))
                    elif name in ("w", "d", "m"):
                        prep((name, g))
                    else:
                        stage(name, g)
                if q >= LAG:
                    down(q - LAG)
            for q in range(SLOTS - LAG, SLOTS):
                down(q)


def hadamard(n):
    import numpy as np

    h = np.ones((1, 1), np.float32)
    while h.shape[0] < n:
        h = np.block([[h, h], [h, -h]])
    return h


def kernel(**inputs):
    import concourse.bacc as bacc
    import numpy as np
    from concourse.bass_utils import run_bass_kernel_spmd

    flat = ("L0_xattn_w", "L0_xattn_u", "L0_ffn_SU_ug", "L0_ffn_SU_dp", "L0_ffn_Wscale_ug", "L0_ffn_Wscale_dp")
    gates = np.concatenate([np.asarray(inputs["g_xattn"]), np.asarray(inputs["g_ffn"])])
    steps = np.kron(np.eye(CT, dtype=np.float32), np.tile(np.arange(P, dtype=np.float32), GB))
    arrays = {
        "x": np.ascontiguousarray(inputs["x"]),
        "ctx": np.ascontiguousarray(inputs["ctx_2048"]),
        "vecs": np.concatenate([np.asarray(inputs[n]) for n in flat]).reshape(NV, P),
        "consts": np.ascontiguousarray(np.concatenate([hadamard(P), np.eye(P, dtype=np.float32), np.broadcast_to(gates, (P, 2))], axis=1)),
        "steps": np.concatenate([steps, np.zeros((32 - CT, CT * GT), np.float32), steps]),
        "w_up": np.ascontiguousarray(inputs["L0_ffn_W_up"]),
        "w_gate": np.ascontiguousarray(inputs["L0_ffn_W_gate"]),
        "w_down": np.ascontiguousarray(inputs["L0_ffn_W_down"]),
    }
    nc = bacc.Bacc("TRN2", target_bir_lowering=False, num_devices=1)
    arrays = {f"in_{n}": a for n, a in arrays.items()}
    args = [nc.dram_tensor(n, a.shape, F32, kind="ExternalInput").ap() for n, a in arrays.items()]
    out = nc.dram_tensor("out_0", (NB, P, C), F32, kind="ExternalOutput").ap()
    build(nc, *args, out)
    return run_bass_kernel_spmd(nc, [arrays], core_ids=[0]).results[0]["out_0"]
```

```python
from contextlib import ExitStack

import concourse.bass as bass
from concourse import mybir

F32 = mybir.dt.float32
F32R = mybir.dt.float32r
ALU = mybir.AluOpType
ACT = mybir.ActivationFunctionType

P = 128
NB = 8
C = 256
INTER = 1024
CT = C // P
JT = INTER // P
GB = 2
NG = NB // GB
GT = GB * P
PAD = P + 1
SLOTS = NG * JT
EPS = 1e-5
C_MAX, C_MIN = 56.0, -50.0
M_NEG, M_POS = 0.45, 0.05
SCALE_UG = C ** -0.5
SCALE_DP = INTER ** -0.5

V_W, V_U, V_SUG, V_SDP, V_SUP, V_SGATE = 0, 2, 4, 6, 14, 22
NV = 30

NBANKS = 4
LAG = 6
RING = 4

PE_STAGES = {
    -1: [("keys", 0), ("values", 0), ("w", 2), ("w", 0), ("w_rest", 2), ("w_rest", 0), ("w", 3), ("w", 1), ("w_rest", 1), ("y", 0),
         ("w", 4), ("w_rest", 3), ("w", 6), ("w_rest", 4), ("w", 7), ("keys", 1), ("w", 5), ("w_rest", 6), ("turn", 0), ("w_rest", 5),
         ("w_rest", 7), ("fwht", 0), ("keys", 2), ("values", 1), ("d", 2), ("d", 0)], 0: [("d", 1)], 2: [("d", 3), ("y", 1), ("m", 2)],
    3: [("m", 0)], 5: [("m", 3), ("m", 1), ("turn", 1)], 7: [("fwht", 1), ("keys", 3)], 8: [("values", 2)], 11: [("y", 2)],
    13: [("turn", 2)], 14: [("fwht", 2)], 15: [("values", 3)], 18: [("y", 3)], 20: [("turn", 3)], 22: [("fwht", 3)]}
ACT_STAGES = {
    -1: [("setup", 0), ("keys", 0), ("w_hi", 2), ("w_hi", 0), ("w_lo", 2), ("recip", 0), ("w_hi", 1), ("w_lo", 0), ("w_lo", 1),
         ("scales", 0), ("w_hi", 3), ("w_hi", 4), ("w_lo", 3), ("w_lo", 4), ("w_hi", 6), ("w_hi", 7), ("keys", 1), ("w_hi", 5),
         ("w_lo", 6), ("turn", 0), ("w_lo", 5), ("w_lo", 7), ("fwht", 0), ("recip", 1), ("keys", 2), ("silu_table", 0), ("round", 2)],
    0: [("round", 0)], 2: [("round", 1), ("m_hi", 2), ("round", 3)], 3: [("m_hi", 0)], 5: [("m_hi", 3), ("m_hi", 1), ("turn", 1)],
    7: [("fwht", 1), ("exp_block", (("recip", 2), ("keys", 3)))], 11: [("exp_block", (("recip", 3),))], 12: [("turn", 2)],
    14: [("fwht", 2)], 20: [("turn", 3)], 22: [("fwht", 3)]}
DVE_STAGES = {
    -1: [("stats1", 0), ("setup_rows", 0), ("norm1", 0), ("setup_shift", 0), ("scan_a", 0), ("av", 0), ("mix_den", 0), ("scan_av", 0),
         ("mix_num", 0), ("estimate", 0), ("fly", (1, 0)), ("newton", 0), ("stats1", 1), ("residual", 0), ("stats2", 0), ("norm1", 1),
         ("norm2", 0), ("fly", (1, 3)), ("stats1", 2), ("scan_a", 1), ("fly", (1, 4)), ("turn", 0), ("norm1", 2), ("mix_den", 1),
         ("fwht", 0), ("stats1", 3), ("av", 1), ("d_scaled", 2), ("scan_av", 1), ("d_scaled", 0), ("mix_num", 1)], 0: [("estimate", 1)],
    1: [("newton", 1), ("d_scaled", 1)], 2: [("residual", 1), ("d_scaled", 3), ("stats2", 1), ("m_lo", 2)], 3: [("m_lo", 0)],
    4: [("norm2", 1), ("scan_a", 2)], 5: [("mix_den", 2), ("m_lo", 3), ("turn", 1)], 6: [("m_lo", 1), ("norm1", 3)], 7: [("fwht", 1),
         ("av", 2), ("scan_av", 2), ("mix_num", 2), ("scan_a", 3)], 8: [("estimate", 2)], 9: [("newton", 2)], 10: [("mix_den", 3),
         ("residual", 2)], 11: [("stats2", 2), ("norm2", 2)], 12: [("turn", 2)], 14: [("fwht", 2)], 15: [("av", 3), ("scan_av", 3),
         ("mix_num", 3)], 16: [("estimate", 3), ("newton", 3)], 17: [("residual", 3)], 18: [("stats2", 3)], 19: [("norm2", 3)],
    20: [("turn", 3)], 22: [("fwht", 3)]}
POOL_STAGES = {
    -1: [("rstd1", 0), ("setup", 0), ("fly", (0, 1)), ("fly", (0, 0)), ("error", 0), ("fly", (0, 2)), ("rstd1", 1), ("fly", (1, 1)),
         ("rstd2", 0), ("fly", (1, 2)), ("fly", (1, 5)), ("rstd1", 2), ("fly", (0, 3)), ("fly", (0, 4)), ("fly", (0, 5)), ("error", 1),
         ("rstd1", 3), ("rest", 2), ("rest", 0)], 1: [("rest", 1), ("rstd2", 1), ("rest", 3)], 6: [("error", 2)], 10: [("rstd2", 2),
         ("error", 3)], 17: [("rstd2", 3)]}


def stages(table):
    return [item for q in range(-1, SLOTS) for item in table.get(q, [])]


ORDER = []
for q in range(-1, SLOTS):
    if q >= 0:
        ORDER.append(("up", q))
    ORDER += [item for item in PE_STAGES.get(q, []) if item[0] in ("w", "d", "m")]
INDEX = {item: n for n, item in enumerate(ORDER)}
KZ_FILLS = [item for item in stages(PE_STAGES) if item[0] in ("keys", "turn")]
VX_FILLS = [item for item in stages(PE_STAGES) if item[0] in ("values", "fwht")]
HI_ON_ACT = [(name[0], n) for name, n in stages(ACT_STAGES) if name.endswith("_hi")]
LO_ON_ACT = [(name[0], n) for name, n in stages(ACT_STAGES) if name.endswith("_lo")]
ROUNDED = [n for name, n in stages(ACT_STAGES) if name == "round"]
RESTED = [n for name, n in stages(POOL_STAGES) if name == "rest"]
RESTS = [(name[0], n) for name, n in stages(PE_STAGES) if name.endswith("_rest")]
LO_ON_DVE = [(name[0], n) for name, n in stages(DVE_STAGES) if name.endswith(("_lo", "_scaled"))]


def build(nc, x, ctx, vecs, consts, steps, scales, w_up, w_gate, w_down, out):
    with ExitStack() as stack:
        def sb(name, shape, dt=F32):
            return stack.enter_context(nc.sbuf_tensor(name, shape, dt))

        def bank(name):
            return stack.enter_context(nc.psum_tensor(name, [P, 512], F32))

        def sem(name):
            return stack.enter_context(nc.semaphore(name))

        X = sb("X", [P, NB, C])
        V = sb("V", [P, NB, C])
        VR = sb("VR", [NV, P])
        VT = sb("VT", [P, NV])
        TG = sb("TG", [P, 2])
        HI = sb("HI", [P, 2 * P + 2])
        HP = sb("HP", [P, P], F32R)
        HN = sb("HN", [P, P], F32R)
        NI = sb("NI", [P, P], F32R)
        STEP = sb("STEP", [P, CT, GT])
        STEPR = sb("STEPR", [P, CT, GT], F32R)
        NEGW = sb("NEGW", [CT, P])
        WPLUS = sb("WPLUS", [P, P], F32R)
        DEC = sb("DEC", [P, CT])
        NHALF = sb("NHALF", [P, GB])
        SUMU = sb("SUMU", [P, CT])
        CUR = sb("CUR", [P, CT])
        RATIO = sb("RATIO", [P, CT])
        MPOS = sb("MPOS", [P, CT])
        NEGM = sb("NEGM", [P, CT])
        D = sb("D", [P, CT, GB, PAD])
        ALPHA = sb("ALPHA", [P, JT])
        SROW = sb("SROW", [P, C])
        OUTS = sb("OUTS", [P, 2, C])
        WN = sb("WN", [P, 2, JT, C])
        WTH = sb("WTH", [P, 2, JT, CT, P], F32R)
        WTL = sb("WTL", [P, 2, JT, CT, P], F32R)
        DN = sb("DN", [P, CT, JT, P])
        DB = sb("DB", [P, CT, JT, P])
        DT = DN[:, :, :, :].rearrange("p t j q -> p (t j q)").rearrange("p (j c) -> p j c", c=C)
        DTH = sb("DTH", [P, JT, C], F32R)
        DTL = sb("DTL", [P, JT, C], F32R)
        MH = sb("MH", [P, JT, C], F32R)
        ML = sb("ML", [P, JT, C], F32R)
        BS1, BS2 = (sb(n, [P, GB, 6]) for n in ("BS1", "BS2"))
        MV1, MV2 = (sb(n, [P, GB, 2]) for n in ("MV1", "MV2"))
        VE1, VE2, RS1, RS2 = (sb(n, [P, GB]) for n in ("VE1", "VE2", "RS1", "RS2"))
        XHAT = sb("XHAT", [P, GB, C])
        Z = sb("Z", [P, GB, C])
        EA = sb("EA", [P, NG, CT, GB, PAD])
        EV = sb("EV", [P, NG, CT, GB, PAD])
        SQ = sb("SQ", [P, CT, GB, PAD])
        SP_ = sb("SP_", [P, CT, GB, PAD])
        NUM, DEN, R0, ERR, Y = (sb(n, [P, 2, CT, GB, P]) for n in ("NUM", "DEN", "R0", "ERR", "Y"))
        ZH = sb("ZH", [P, CT, GT], F32R)
        ZL = sb("ZL", [P, CT, GT], F32R)
        FH = sb("FH", [P, 2, CT, GT], F32R)
        FL = sb("FL", [P, 2, CT, GT], F32R)
        S = sb("S", [P, RING, GT])
        H = sb("H", [P, RING, GT])
        HH = sb("HH", [P, JT, GT], F32R)
        HL = sb("HL", [P, JT, GT], F32R)

        UG = [bank(f"UG{i}") for i in range(NBANKS)]
        OD = bank("OD")
        KZ = bank("KZ")
        VX = bank("VX")
        YB = bank("YB")
        IDENT = HI[:, P:2 * P]

        x_in = [sem(f"x{i}_in") for i in range(3)]
        ctx_in = [sem(f"ctx{i}_in") for i in range(3)]
        const_in, vec_in, step_in, scale_in, stored = (sem(n) for n in ("const_in", "vec_in", "step_in", "scale_in", "stored"))
        w_in = {(m, h): sem(f"w{m}{h}_in") for m in range(2) for h in range(2)}
        wd_in = [sem(f"wd{t}_in") for t in range(CT)]
        step_clear, plus_clear, pads, d_clear, half = (sem(n) for n in ("step_clear", "plus_clear", "pads", "d_clear", "half"))
        vecs_turned, vecs_kept, tanh_gate, decay_ready, c_ready, m_ready, ratio_ready, decay_set = (sem(n) for n in (
            "vecs_turned", "vecs_kept", "tanh_gate", "decay_ready", "c_ready", "m_ready", "ratio_ready", "decay_set"))
        consts_r, wplus, steps_r, alpha, outs = (sem(n) for n in ("consts_r", "wplus", "steps_r", "alpha", "outs"))
        bank_full, rest_full = sem("bank_full"), sem("rest_full")
        bank_hi, lo_on_act, bank_read = sem("bank_hi"), sem("lo_on_act"), sem("bank_read")
        d_rounded, d_rest = sem("d_rounded"), sem("d_rest")
        flown = [sem(f"flown{t}") for t in range(CT)]
        stats1, mv1, ve1, rstd1, xhat, k_turned, v_turned, a_ready, av_ready = (sem(n) for n in (
            "stats1", "mv1", "ve1", "rstd1", "xhat", "k_turned", "v_turned", "a_ready", "av_ready"))
        scanned, mixed, ln_ready, r0_ready, err_ready, y0_ready, y_ready, y_turned = (sem(n) for n in (
            "scanned", "mixed", "ln_ready", "r0_ready", "err_ready", "y0_ready", "y_ready", "y_turned"))
        x1_ready, stats2, mv2, ve2, rstd2, z_ready, z_turned, z_hi, z_lo, f_full, f_hi, f_lo = (sem(n) for n in (
            "x1_ready", "stats2", "mv2", "ve2", "rstd2", "z_ready", "z_turned", "z_hi", "z_lo", "f_full", "f_hi", "f_lo"))
        silu_ready, h_ready, h_hi, h_lo, down_full, out_ready = (sem(n) for n in (
            "silu_ready", "h_ready", "h_hi", "h_lo", "down_full", "out_ready"))

        x_v = x.rearrange("b p c -> p b c")
        ctx_v = ctx.rearrange("b p c -> p b c")
        out_v = out.rearrange("b p c -> p b c")

        def total(g, b):
            last = g == NG - 1 and b == GB - 1
            return (VX if last else OD)[:, (0 if last else b * C):(C if last else (b + 1) * C)]

        def fill(item):
            return UG[INDEX[item] % NBANKS]

        def wait_lo(eng, item):
            if item in LO_ON_ACT:
                eng.wait_ge(lo_on_act, LO_ON_ACT.index(item) + 1)
            else:
                eng.wait_ge(bank_read, LO_ON_DVE.index(item) + 1)

        def wait_bank_free(eng, item):
            n = INDEX[item] - NBANKS
            if n >= 0:
                last = ORDER[n]
                if last[0] == "up":
                    eng.wait_ge(h_ready, last[1] + 1)
                else:
                    wait_lo(eng, last)

        def n_hi(item):
            return HI_ON_ACT.index(item) + 1

        def parts(item):
            kind, n = item
            if kind == "w":
                m, j = n % 2, 2 * (n // 2)
                return [t[:, m, j:j + 2, :, :].rearrange("p j t q -> p (j t q)") for t in (WTH, WTL)]
            return [t[:, 2 * n:2 * n + 2, :].rearrange("p j c -> p (j c)") for t in ((DT,) if kind == "d" else (MH, ML))]

        def fly(eng, t, n):
            step = n // 2
            src, dst = (DN, DB) if step % 2 == 0 else (DB, DN)
            s, d = (a[:, t, :, :].rearrange("p (n two h) q -> p n two (h q)", two=2, h=1 << step) for a in (src, dst))
            if step == 0:
                eng.wait_ge(wd_in[t], 16)
            else:
                eng.wait_ge(flown[t], 2 * step)
            eng.tensor_tensor(d[:, :, n % 2, :], s[:, :, 0, :], s[:, :, 1, :], ALU.subtract if n % 2 else ALU.add).then_inc(flown[t], 1)

        def arrival(g):
            return min(g, 2)

        block = stack.enter_context(nc.Block())

        @block.sync
        def _(sp):
            def load_x(i):
                b = slice(GB * i, GB * (i + 1) if i < 2 else NB)
                sp.dma_start(X[:, b, :], x_v[:, b, :]).then_inc(x_in[i], 16)

            def load_ctx(i):
                b = slice(GB * i, GB * (i + 1) if i < 2 else NB)
                sp.dma_start(V[:, b, :], ctx_v[:, b, :]).then_inc(ctx_in[i], 16)

            load_x(0)
            sp.dma_start(VR[:, :], vecs).then_inc(vec_in, 16)
            sp.dma_start(HI[:, :], consts).then_inc(const_in, 16)
            sp.wait_ge(step_clear, 1)
            sp.dma_start(STEP[0:32 + CT, :, :].rearrange("p t n -> p (t n)"), steps).then_inc(step_in, 16)
            load_ctx(0)

            def load_w(m, h):
                j = slice(h * JT // 2, (h + 1) * JT // 2)
                sp.dma_start(WN[:, m, j, :], (w_gate, w_up)[m].rearrange("(t p) c -> p t c", p=P)[:, j, :]).then_inc(w_in[m, h], 16)

            def load_down(t):
                sp.dma_start(DN[:, t, :, :], w_down.rearrange("(t p) (j q) -> p t j q", p=P, q=P)[:, t, :, :]).then_inc(wd_in[t], 16)

            load_w(0, 0)
            load_down(0)
            sp.dma_start(SROW[:, :], scales).then_inc(scale_in, 16)
            load_w(1, 0)
            load_down(1)
            load_x(1)
            load_ctx(1)
            load_w(0, 1)
            load_w(1, 1)
            load_x(2)
            load_ctx(2)
            leaving = [slice(GB * g, GB * (g + 1)) for g in range(NG - 1)] + [slice(b, b + 1) for b in range(NB - GB, NB)]
            for n, b in enumerate(leaving):
                sp.wait_ge(out_ready, n + 1)
                sp.dma_start(out_v[:, b, :], X[:, b, :]).then_inc(stored, 16)
            sp.wait_ge(stored, 16 * len(leaving))

        @block.gpsimd
        def _(pool):
            pool.memset(STEP[:, :, :], 0.0).then_inc(step_clear, 1)
            pool.memset(WPLUS[:, :].bitcast(F32), 0.0).then_inc(plus_clear, 1)
            pool.memset(NHALF[:, :], -0.5).then_inc(half, 1)
            pool.memset(D[:, :, :, :], 0.0).then_inc(d_clear, 1)
            pool.memset(EA[:, :, :, :, 0:1], 0.0).then_inc(pads, 1)
            pool.memset(EV[:, :, :, :, 0:1], 0.0).then_inc(pads, 1)

            def stage(name, g):
                if name == "setup":
                    pool.wait_ge(d_clear, 1)
                    pool.wait_ge(decay_ready, 2)
                    for t in range(CT):
                        pool.tensor_scalar(D[:, t, :, 1:PAD], D[:, t, :, 1:PAD], 1.0, DEC[:, t:t + 1], ALU.mult, ALU.add).then_inc(decay_set, 1)
                    pool.wait_ge(vecs_kept, 1)
                    pool.tensor_scalar(ALPHA[:, :], VT[:, V_SUP:V_SUP + JT], SCALE_DP, 1.0, ALU.mult, ALU.mult).then_inc(alpha, 1)
                    pool.wait_ge(alpha, 1)
                    pool.tensor_tensor(ALPHA[:, :], ALPHA[:, :], VT[:, V_SDP:V_SDP + JT], ALU.mult).then_inc(alpha, 1)
                elif name in ("rstd1", "rstd2"):
                    ve, VE, rstd, RS = (ve1, VE1, rstd1, RS1) if name == "rstd1" else (ve2, VE2, rstd2, RS2)
                    pool.wait_ge(half, 1)
                    pool.wait_ge(ve, g + 1)
                    pool.tensor_tensor(RS[:, :], VE[:, :], NHALF[:, :], ALU.pow).then_inc(rstd, 1)
                elif name == "error":
                    pool.wait_ge(r0_ready, g + 1)
                    pool.tensor_tensor(ERR[:, g % 2, :, :, :], DEN[:, g % 2, :, :, :], R0[:, g % 2, :, :, :], ALU.mult).then_inc(err_ready, 1)
                elif name == "rest":
                    pool.wait_ge(d_rounded, ROUNDED.index(g) + 1)
                    tiles = slice(2 * g, 2 * g + 2)
                    pool.tensor_tensor(DTL[:, tiles, :], DT[:, tiles, :], DTH[:, tiles, :].bitcast(F32), ALU.subtract).then_inc(d_rest, 1)
                elif name == "fly":
                    fly(pool, *g)

            for q in range(-1, SLOTS):
                if q >= 0:
                    pool.wait_ge(h_hi, q + 1)
                    pool.tensor_tensor(HL[:, q % JT, :], H[:, q % RING, :], HH[:, q % JT, :].bitcast(F32), ALU.subtract).then_inc(h_lo, 1)
                for name, g in POOL_STAGES.get(q, []):
                    stage(name, g)

        @block.scalar
        def _(act):
            def keys(g):
                act.wait_ge(k_turned, g + 1)
                if g == 0:
                    act.wait_ge(m_ready, 2)
                    act.wait_ge(pads, 1)
                for t in range(CT):
                    i = act.activation(EA[:, g, t, :, 1:PAD], KZ[:, t * GT:(t + 1) * GT].rearrange("p (b q) -> p b q", b=GB),
                                       ACT.Exp, bias=NEGM[:, t:t + 1])
                i.then_inc(a_ready, 1)

            def reciprocal(g):
                act.wait_ge(mixed, 2 * g + 1)
                act.activation(R0[:, g % 2, :, :, :], DEN[:, g % 2, :, :, :], ACT.Ln).then_inc(ln_ready, 1)
                act.wait_ge(ln_ready, g + 1)
                act.activation(R0[:, g % 2, :, :, :], R0[:, g % 2, :, :, :], ACT.Exp, scale=-1.0).then_inc(r0_ready, 1)

            def stage(name, g):
                if name == "setup":
                    act.preload_act_table_set("exp_and_others")
                    act.wait_ge(const_in, 16)
                    act.activation(TG[:, 0:1], HI[:, 2 * P:2 * P + 1], ACT.Tanh, scale=-1.0).then_inc(tanh_gate, 1)
                    act.activation(TG[:, 1:2], HI[:, 2 * P + 1:2 * P + 2], ACT.Tanh).then_inc(tanh_gate, 1)
                    act.preload_act_table_set("natural_log_exp_and_others")
                    act.activation(HP[:, :], HI[:, 0:P], ACT.Copy).then_inc(consts_r, 1)
                    act.activation(HN[:, :], HI[:, 0:P], ACT.Copy, scale=-1.0).then_inc(consts_r, 1)
                    act.activation(NI[:, :], IDENT, ACT.Copy, scale=-1.0).then_inc(consts_r, 1)
                    act.wait_ge(step_in, 16)
                    act.activation(STEPR[:, :, :], STEP[:, :, :], ACT.Copy).then_inc(steps_r, 1)
                    act.wait_ge(decay_ready, 1)
                    act.activation(DEC[:, :], DEC[:, :], ACT.Exp).then_inc(decay_ready, 1)
                    act.wait_ge(c_ready, 3)
                    act.activation(RATIO[:, :], CUR[:, :], ACT.Exp).then_inc(ratio_ready, 1)
                elif name == "keys":
                    keys(g)
                elif name == "recip":
                    reciprocal(g)
                elif name == "silu_table":
                    act.preload_act_table_set("silu_and_others")
                elif name == "exp_block":
                    act.preload_act_table_set("natural_log_exp_and_others")
                    for part in g:
                        stage(*part)
                    act.preload_act_table_set("silu_and_others")
                elif name == "round":
                    wait_lo(act, ("d", g))
                    act.activation(DTH[:, 2 * g:2 * g + 2, :], DT[:, 2 * g:2 * g + 2, :], ACT.Copy).then_inc(d_rounded, 1)
                elif name == "scales":
                    act.wait_ge(scale_in, 16)
                    act.wait_ge(tanh_gate, 2)
                    for n in range(2):
                        act.activation(OUTS[:, n, :], SROW[:, :], ACT.Copy, scale=TG[:, 1:2]).then_inc(outs, 1)
                elif name.endswith("_hi"):
                    item = (name[0], g)
                    act.wait_ge(bank_full, INDEX[item] + 1)
                    act.activation(parts(item)[0], fill(item)[:, :], ACT.Copy).then_inc(bank_hi, 1)
                elif name.endswith("_lo"):
                    item = (name[0], g)
                    act.wait_ge(rest_full, RESTS.index(item) + 1)
                    act.activation(parts(item)[1], fill(item)[:, :], ACT.Copy).then_inc(lo_on_act, 1)
                elif name == "turn":
                    act.wait_ge(z_turned, g + 1)
                    if g:
                        act.wait_ge(f_full, g)
                    for t in range(CT):
                        act.activation(ZH[:, t, :], KZ[:, t * GT:(t + 1) * GT], ACT.Copy, scale=VT[:, V_SUG + t:V_SUG + t + 1]).then_inc(z_hi, 1)
                elif name == "fwht":
                    act.wait_ge(f_full, g + 1)
                    act.activation(FH[:, g % 2, :, :], VX[:, :].rearrange("p (t n) -> p t n", t=CT), ACT.Copy, scale=SCALE_UG).then_inc(f_hi, 1)

            def hi(q):
                act.wait_ge(h_ready, q + 1)
                act.activation(HH[:, q % JT, :], H[:, q % RING, :], ACT.Copy).then_inc(h_hi, 1)

            def gate(q):
                j = q % JT
                act.wait_ge(bank_full, INDEX["up", q] + 1)
                act.activation(S[:, q % RING, :], fill(("up", q))[:, 0:GT], ACT.Silu, scale=VT[:, V_SGATE + j:V_SGATE + j + 1]).then_inc(silu_ready, 1)
                if q:
                    hi(q - 1)

            for q in range(-1, SLOTS):
                if q >= 0:
                    gate(q)
                for name, g in ACT_STAGES.get(q, []):
                    stage(name, g)
            hi(SLOTS - 1)

        @block.vector
        def _(dve):
            def statistics(g, BS, stats, MV, mv, VE, ve):
                for b in range(GB):
                    dve.bn_stats(BS[:, b, :], X[:, GB * g + b, :]).then_inc(stats, 1)
                dve.wait_ge(stats, (g + 1) * GB)
                for b in range(GB):
                    i = dve.bn_aggr(MV[:, b, :], BS[:, b, :])
                i.then_inc(mv, 1)
                dve.wait_ge(mv, g + 1)
                dve.tensor_scalar(VE[:, :], MV[:, :, 1], EPS, None, ALU.add).then_inc(ve, 1)

            def normalise(g, dst, MV, RS, rstd, ready):
                dve.wait_ge(rstd, g + 1)
                for b in range(GB):
                    i = dve.tensor_scalar(dst[:, b, :], X[:, GB * g + b, :], MV[:, b, 0:1], RS[:, b:b + 1], ALU.subtract, ALU.mult)
                i.then_inc(ready, 1)

            def stage(name, g):
                if name == "stats1":
                    dve.wait_ge(x_in[arrival(g)], 16)
                    if g:
                        dve.wait_ge(xhat, g)
                    statistics(g, BS1, stats1, MV1, mv1, VE1, ve1)
                elif name == "norm1":
                    if g:
                        dve.wait_ge(k_turned, g)
                    normalise(g, XHAT, MV1, RS1, rstd1, xhat)
                elif name == "av":
                    if g == 0:
                        dve.wait_ge(pads, 2)
                    dve.wait_ge(v_turned, g + 1)
                    dve.wait_ge(a_ready, g + 1)
                    dve.tensor_tensor(EV[:, g, :, :, 1:PAD].rearrange("p t b q -> p (t b) q"), EA[:, g, :, :, 1:PAD].rearrange("p t b q -> p (t b) q"),
                                      VX[:, :].rearrange("p (n q) -> p n q", q=P), ALU.mult).then_inc(av_ready, 1)
                elif name in ("scan_a", "scan_av"):
                    n, ready, src, dst = (0, a_ready, EA, SQ) if name == "scan_a" else (1, av_ready, EV, SP_)
                    if g == 0:
                        dve.wait_ge(decay_set, 2)
                    else:
                        dve.wait_ge(mixed, 2 * g - 1 + n)
                    dve.wait_ge(ready, g + 1)
                    flat = "p t b q -> p (t b q)"
                    dve.tensor_tensor_scan(dst[:, :, :, :].rearrange(flat), D[:, :, :, :].rearrange(flat), src[:, g, :, :, :].rearrange(flat),
                                           0.0, ALU.mult, ALU.add).then_inc(scanned, 1)
                elif name in ("mix_den", "mix_num"):
                    n, dst, cur, state = (0, DEN, EA, SQ) if name == "mix_den" else (1, NUM, EV, SP_)
                    if g == 0:
                        dve.wait_ge(ratio_ready, 1)
                    elif g > 1:
                        dve.wait_ge(y_ready, g - 1)
                    dve.wait_ge(scanned, 2 * g + n + 1)
                    for t in range(CT):
                        i = dve.scalar_tensor_tensor(out=dst[:, g % 2, t, :, :], in0=cur[:, g, t, :, 1:PAD], scalar=RATIO[:, t:t + 1],
                                                     in1=state[:, t, :, 0:P], op0=ALU.mult, op1=ALU.add)
                    i.then_inc(mixed, 1)
                elif name == "error":
                    dve.wait_ge(r0_ready, g + 1)
                    dve.tensor_tensor(ERR[:, g % 2, :, :, :], DEN[:, g % 2, :, :, :], R0[:, g % 2, :, :, :], ALU.mult).then_inc(err_ready, 1)
                elif name == "estimate":
                    dve.wait_ge(r0_ready, g + 1)
                    dve.wait_ge(mixed, 2 * g + 2)
                    if g > 1:
                        dve.wait_ge(y_turned, g - 1)
                    dve.tensor_tensor(Y[:, g % 2, :, :, :], NUM[:, g % 2, :, :, :], R0[:, g % 2, :, :, :], ALU.mult).then_inc(y0_ready, 1)
                elif name == "newton":
                    dve.wait_ge(err_ready, g + 1)
                    dve.wait_ge(y0_ready, g + 1)
                    dve.scalar_tensor_tensor(out=Y[:, g % 2, :, :, :].rearrange("p t b q -> p (t b q)"), in0=ERR[:, g % 2, :, :, :].rearrange("p t b q -> p (t b q)"),
                                             scalar=2.0, in1=Y[:, g % 2, :, :, :].rearrange("p t b q -> p (t b q)"), op0=ALU.subtract,
                                             op1=ALU.mult).then_inc(y_ready, 1)
                elif name == "residual":
                    dve.wait_ge(y_turned, g + 1)
                    xg = X[:, GB * g:GB * (g + 1), :]
                    dve.scalar_tensor_tensor(out=xg, in0=YB[:, :].rearrange("p (b c) -> p b c", b=GB), scalar=TG[:, 0:1], in1=xg,
                                             op0=ALU.mult, op1=ALU.add).then_inc(x1_ready, 1)
                elif name == "stats2":
                    if g:
                        dve.wait_ge(z_ready, g)
                    dve.wait_ge(x1_ready, g + 1)
                    statistics(g, BS2, stats2, MV2, mv2, VE2, ve2)
                elif name == "norm2":
                    if g:
                        dve.wait_ge(z_turned, g)
                    normalise(g, Z, MV2, RS2, rstd2, z_ready)
                elif name == "turn":
                    dve.wait_ge(z_hi, CT * (g + 1))
                    for t in range(CT):
                        i = dve.scalar_tensor_tensor(out=ZL[:, t, :], in0=KZ[:, t * GT:(t + 1) * GT], scalar=VT[:, V_SUG + t:V_SUG + t + 1],
                                                     in1=ZH[:, t, :].bitcast(F32), op0=ALU.mult, op1=ALU.subtract)
                    i.then_inc(z_lo, 1)
                elif name == "fwht":
                    dve.wait_ge(f_hi, g + 1)
                    dve.scalar_tensor_tensor(out=FL[:, g % 2, :, :].rearrange("p t n -> p (t n)"), in0=VX[:, :], scalar=SCALE_UG,
                                             in1=FH[:, g % 2, :, :].rearrange("p t n -> p (t n)").bitcast(F32),
                                             op0=ALU.mult, op1=ALU.subtract).then_inc(f_lo, 1)
                elif name == "fly":
                    fly(dve, *g)
                elif name == "d_scaled":
                    dve.wait_ge(outs, 2)
                    dve.wait_ge(bank_full, INDEX["d", g] + 1)
                    dve.tensor_tensor(parts(("d", g))[0], fill(("d", g))[:, :], OUTS[:, :, :].rearrange("p n c -> p (n c)"), ALU.mult).then_inc(bank_read, 1)
                elif name.endswith("_lo"):
                    item = (name[0], g)
                    dve.wait_ge(bank_hi, n_hi(item))
                    hi, lo = parts(item)
                    dve.tensor_tensor(lo, fill(item)[:, :], hi.bitcast(F32), ALU.subtract).then_inc(bank_read, 1)

            def setup_rows():
                dve.wait_ge(vecs_turned, 1)
                dve.tensor_copy(VT[:, :], YB[:, 0:NV]).then_inc(vecs_kept, 1)
                dve.wait_ge(vec_in, 16)
                dve.tensor_scalar(NEGW[:, :], VR[V_W:V_W + CT, :], 0.0, -1.0, ALU.max, ALU.mult).then_inc(wplus, 1)
                dve.wait_ge(wplus, 1)
                dve.wait_ge(plus_clear, 1)
                dve.tensor_copy(WPLUS[0:CT, :], NEGW[:, :]).then_inc(wplus, 1)
                dve.wait_ge(vecs_kept, 1)
                dve.tensor_scalar(DEC[:, :], VT[:, V_W:V_W + CT], 0.0, None, ALU.min).then_inc(decay_ready, 1)
                dve.wait_ge(wplus, 2)
                dve.tensor_tensor(WPLUS[32:32 + CT, :], NEGW[:, :], WPLUS[0:CT, :].bitcast(F32), ALU.subtract).then_inc(wplus, 1)

            def setup_shift():
                dve.tensor_scalar(SUMU[:, :], VT[:, V_W:V_W + CT], 0.0, None, ALU.max).then_inc(c_ready, 1)
                dve.wait_ge(c_ready, 1)
                dve.tensor_tensor(SUMU[:, :], SUMU[:, :], VT[:, V_U:V_U + CT], ALU.add).then_inc(c_ready, 1)
                dve.wait_ge(c_ready, 2)
                dve.tensor_scalar(CUR[:, :], SUMU[:, :], C_MAX, C_MIN, ALU.min, ALU.max).then_inc(c_ready, 1)
                dve.wait_ge(c_ready, 3)
                dve.tensor_scalar(MPOS[:, :], CUR[:, :], 0.0, -M_POS, ALU.max, ALU.mult).then_inc(m_ready, 1)
                dve.wait_ge(m_ready, 1)
                dve.scalar_tensor_tensor(out=NEGM[:, :], in0=CUR[:, :], scalar=-M_NEG, in1=MPOS[:, :], op0=ALU.mult, op1=ALU.add).then_inc(m_ready, 1)

            def out(g):
                dve.wait_ge(down_full, g + 1)
                xg = X[:, GB * g:GB * (g + 1), :]
                dve.tensor_tensor(xg, OD[:, :].rearrange("p (b c) -> p b c", b=GB), xg, ALU.add).then_inc(out_ready, 1)

            def hidden(q):
                j = q % JT
                dve.wait_ge(silu_ready, q + 1)
                if q == 0:
                    dve.wait_ge(alpha, 2)
                if q >= RING:
                    dve.wait_ge(h_lo, q - RING + 1)
                dve.scalar_tensor_tensor(out=H[:, q % RING, :], in0=S[:, q % RING, :], scalar=ALPHA[:, j:j + 1], in1=fill(("up", q))[:, GT:2 * GT],
                                         op0=ALU.mult, op1=ALU.mult).then_inc(h_ready, 1)

            for q in range(-1, SLOTS):
                if q >= JT + LAG and (q - LAG) % JT == 0:
                    out((q - LAG) // JT - 1)
                if q >= 0:
                    hidden(q)
                for name, g in DVE_STAGES.get(q, []):
                    if name == "setup_rows":
                        setup_rows()
                    elif name == "setup_shift":
                        setup_shift()
                    else:
                        stage(name, g)
            for b in range(GB):
                dve.wait_ge(down_full, NG + b)
                xb = X[:, GB * (NG - 1) + b, :]
                dve.tensor_tensor(xb, total(NG - 1, b), xb, ALU.add).then_inc(out_ready, 1)

        @block.tensor
        def _(pe):
            def wait_read(item, fills):
                n = fills.index(item)
                if n:
                    name, g = fills[n - 1]
                    pe.wait_ge({"keys": a_ready, "turn": z_lo, "values": av_ready, "fwht": f_lo}[name], g + 1)

            def stage(name, g):
                if name == "keys":
                    wait_read(("keys", g), KZ_FILLS)
                    pe.wait_ge(xhat, g + 1)
                    for t in range(CT):
                        for b in range(GB):
                            pe.matmul(KZ[:, t * GT + b * P:t * GT + (b + 1) * P], XHAT[:, b, t * P:(t + 1) * P], IDENT, is_transpose=True,
                                      start=(t == 0 and b == 0), stop=False, skip_group_check=True)
                    if g == 0:
                        pe.wait_ge(wplus, 3)
                        pe.wait_ge(steps_r, 1)
                    for t in range(CT):
                        i = pe.matmul(KZ[:, t * GT:(t + 1) * GT], WPLUS[:, :], STEPR[:, t, :], start=False, stop=True, skip_group_check=True)
                    i.then_inc(k_turned, 1)
                elif name == "values":
                    pe.wait_ge(ctx_in[arrival(g)], 16)
                    wait_read(("values", g), VX_FILLS)
                    for t in range(CT):
                        for b in range(GB):
                            i = pe.transpose(VX[:, t * GT + b * P:t * GT + (b + 1) * P], V[:, GB * g + b, t * P:(t + 1) * P], IDENT)
                    i.then_inc(v_turned, 1)
                elif name == "y":
                    pe.wait_ge(y_ready, g + 1)
                    if g:
                        pe.wait_ge(x1_ready, g)
                    for b in range(GB):
                        for t in range(CT):
                            i = pe.transpose(YB[:, b * C + t * P:b * C + (t + 1) * P], Y[:, g % 2, t, b, :], IDENT)
                    i.then_inc(y_turned, 1)
                elif name == "turn":
                    wait_read(("turn", g), KZ_FILLS)
                    pe.wait_ge(z_ready, g + 1)
                    for t in range(CT):
                        for b in range(GB):
                            i = pe.transpose(KZ[:, t * GT + b * P:t * GT + (b + 1) * P], Z[:, b, t * P:(t + 1) * P], IDENT)
                    i.then_inc(z_turned, 1)
                elif name == "fwht":
                    wait_read(("fwht", g), VX_FILLS)
                    pe.wait_ge(consts_r, 2)
                    for o in range(CT):
                        for n, part in enumerate((ZH, ZL)):
                            if n == 1 and o == 0:
                                pe.wait_ge(z_lo, g + 1)
                            for t in range(CT):
                                if n == 0 and o == 0:
                                    pe.wait_ge(z_hi, CT * g + t + 1)
                                i = pe.matmul(VX[:, o * GT:(o + 1) * GT], (HN if o and t else HP)[:, :], part[:, t, :],
                                              start=(n == 0 and t == 0), stop=(n == 1 and t == CT - 1))
                    i.then_inc(f_full, 1)

            def prep(item):
                kind, n = item
                wait_bank_free(pe, item)
                if kind == "m":
                    pe.wait_ge(consts_r, 1)
                    pe.wait_ge(d_rest, RESTED.index(n) + 1)
                    for h, part in enumerate((DTH, DTL)):
                        i = pe.matmul(fill(item)[:, :], HP[:, :], part[:, 2 * n:2 * n + 2, :].rearrange("p j c -> p (j c)"), start=(h == 0), stop=(h == 1))
                    i.then_inc(bank_full, 1)
                    return
                m, j0 = n % 2, 2 * (n // 2)
                if kind == "w":
                    pe.wait_ge(w_in[m, j0 // (JT // 2)], 16)
                else:
                    for t in range(CT):
                        pe.wait_ge(flown[t], 6)
                for i in range(2):
                    for t in range(CT):
                        o = (i * CT + t) * P
                        src = WN[:, m, j0 + i, t * P:(t + 1) * P] if kind == "w" else DB[:, t, 2 * n + i, :]
                        a = pe.transpose(fill(item)[:, o:o + P], src, IDENT) if item not in LO_ON_ACT else pe.matmul(
                            fill(item)[:, o:o + P], src, IDENT, is_transpose=True, start=(o == 0), stop=False, skip_group_check=True)
                a.then_inc(bank_full, 1)

            def take_hi_off(item):
                pe.wait_ge(bank_hi, n_hi(item))
                pe.wait_ge(consts_r, 3)
                pe.matmul(fill(item)[:, :], NI[:, :], parts(item)[0], start=False, stop=True, skip_group_check=True).then_inc(rest_full, 1)

            def up(q):
                g, j = divmod(q, JT)
                item = ("up", q)
                wait_bank_free(pe, item)
                if j == 0:
                    pe.wait_ge(f_hi, g + 1)
                fresh = q < JT and j % 2 == 0
                if fresh:
                    pe.wait_ge(bank_hi, max(n_hi(("w", j)), n_hi(("w", j + 1))))
                for n, (w, f) in enumerate(((WTH, FH), (WTL, FH), (WTH, FL))):
                    if n == 1 and fresh:
                        wait_lo(pe, ("w", j))
                        wait_lo(pe, ("w", j + 1))
                    if n == 2 and j == 0:
                        pe.wait_ge(f_lo, g + 1)
                    for m in range(2):
                        for t in range(CT):
                            a = pe.matmul(fill(item)[:, m * GT:(m + 1) * GT], w[:, m, j, t, :], f[:, g % 2, t, :],
                                          start=(n == m == t == 0), stop=(n == 2 and t == CT - 1), skip_group_check=True)
                a.then_inc(bank_full, 1)

            def down(q):
                g, j = divmod(q, JT)
                pe.wait_ge(h_lo, q + 1)
                if j == 0 and g:
                    pe.wait_ge(out_ready, g)
                if q < JT and j % 2 == 0:
                    wait_lo(pe, ("m", j // 2))
                for b in range(GB):
                    for n, (h, m) in enumerate(((HH, MH), (HH, ML), (HL, MH))):
                        a = pe.matmul(total(g, b), h[:, j, b * P:(b + 1) * P], m[:, j, :],
                                      start=(j == 0 and n == 0 and (b == 0 or g == NG - 1)), stop=(j == JT - 1 and n == 2), skip_group_check=True)
                    if j == JT - 1 and (b == GB - 1 or g == NG - 1):
                        a.then_inc(down_full, 1)

            pe.wait_ge(const_in, 16)
            pe.wait_ge(vec_in, 16)
            pe.transpose(YB[:, 0:NV], VR[:, :], HI[0:NV, P:P + NV]).then_inc(vecs_turned, 1)
            for q in range(-1, SLOTS):
                if q >= 0:
                    up(q)
                for name, g in PE_STAGES.get(q, []):
                    if name == "w_rest":
                        take_hi_off(("w", g))
                    elif name in ("w", "d", "m"):
                        prep((name, g))
                    else:
                        stage(name, g)
                if q >= LAG:
                    down(q - LAG)
            for q in range(SLOTS - LAG, SLOTS):
                down(q)


def hadamard(n):
    import numpy as np

    h = np.ones((1, 1), np.float32)
    while h.shape[0] < n:
        h = np.block([[h, h], [h, -h]])
    return h


def kernel(**inputs):
    import concourse.bacc as bacc
    import numpy as np
    from concourse.bass_utils import run_bass_kernel_spmd

    flat = ("L0_xattn_w", "L0_xattn_u", "L0_ffn_SU_ug", "L0_ffn_SU_dp", "L0_ffn_Wscale_ug")
    gates = np.concatenate([np.asarray(inputs["g_xattn"]), np.asarray(inputs["g_ffn"])])
    steps = np.kron(np.eye(CT, dtype=np.float32), np.tile(np.arange(P, dtype=np.float32), GB))
    arrays = {
        "x": np.ascontiguousarray(inputs["x"]),
        "ctx": np.ascontiguousarray(inputs["ctx_2048"]),
        "vecs": np.concatenate([np.asarray(inputs[n]) for n in flat]).reshape(NV, P),
        "consts": np.ascontiguousarray(np.concatenate([hadamard(P), np.eye(P, dtype=np.float32), np.broadcast_to(gates, (P, 2))], axis=1)),
        "steps": np.concatenate([steps, np.zeros((32 - CT, CT * GT), np.float32), steps]),
        "scales": np.ascontiguousarray(np.broadcast_to(np.asarray(inputs["L0_ffn_Wscale_dp"]), (P, C))),
        "w_up": np.ascontiguousarray(inputs["L0_ffn_W_up"]),
        "w_gate": np.ascontiguousarray(inputs["L0_ffn_W_gate"]),
        "w_down": np.ascontiguousarray(inputs["L0_ffn_W_down"]),
    }
    nc = bacc.Bacc("TRN2", target_bir_lowering=False, num_devices=1)
    arrays = {f"in_{n}": a for n, a in arrays.items()}
    args = [nc.dram_tensor(n, a.shape, F32, kind="ExternalInput").ap() for n, a in arrays.items()]
    out = nc.dram_tensor("out_0", (NB, P, C), F32, kind="ExternalOutput").ap()
    build(nc, *args, out)
    return run_bass_kernel_spmd(nc, [arrays], core_ids=[0]).results[0]["out_0"]
```
